# Optimizing a Trainium2 kernel written in Bass

```python
import numpy as np
import jax
import jax.numpy as jnp

def _softmax(x, axis=-1):
    return jax.nn.softmax(x, axis=axis)

def _gelu(x):
    return jax.nn.gelu(x, approximate=True)

def _silu(x):
    return jax.nn.silu(x)

def _sigmoid(x):
    return jax.nn.sigmoid(x)

def _layernorm(x, axis=-1, eps=1e-05):
    m = jnp.mean(x, axis=axis, keepdims=True)
    v = jnp.var(x, axis=axis, keepdims=True)
    return (x - m) / jnp.sqrt(v + eps)

def _scatter_add(tgt, idx, src, axis=0):
    return tgt.at[idx].add(src)

def _segment_sum(src, seg, n):
    return jax.ops.segment_sum(src, seg, n)
kernel_name = 'mk_cond_seq_d1_seqx_r8_dcaeb8'

def setup_inputs(seed: int=0):
    np.random.seed(seed)
    _w = jnp.asarray

    def _rec_inputs():
        import jax
        import jax.numpy as jnp
        _rk = jax.random.key(seed)
        x = 3.843e-05 + 0.9999 * jax.random.normal(jax.random.fold_in(_rk, 1), (32, 128, 128), jnp.float32)
        _lenS = 128 - jax.random.randint(jax.random.fold_in(_rk, 7), (32,), 0, max(1, 128 // 4) + 1, jnp.int32)
        _lenS2 = 128 - jax.random.randint(jax.random.fold_in(_rk, 8), (32,), 0, max(1, 128 // 4) + 1, jnp.int32)
        fside_BxS_0 = 0.0125939 + 0.993166 * jax.random.normal(jax.random.fold_in(_rk, 11), (32, 128), jnp.float32)
        cond_1024 = 0.00516053 + 0.988656 * jax.random.normal(jax.random.fold_in(_rk, 12), (32, 128), jnp.float32)
        return (x, fside_BxS_0, cond_1024)
    x, fside_BxS_0, cond_1024 = _rec_inputs()

    def _L0_cond_setup():
        import jax, jax.numpy as jnp
        import numpy as np
        B, S, D = (8, 128, 128)
        EPS = 1e-05

        def _layernorm(h, g, b):
            mu = jnp.mean(h, axis=-1, keepdims=True)
            var = jnp.mean((h - mu) ** 2, axis=-1, keepdims=True)
            return (h - mu) * jax.lax.rsqrt(var + EPS) * g + b
        key = jax.random.key(seed)
        ks = jax.random.split(key, 16)

        def lin(k, fan_in, fan_out):
            bound = 1.0 / np.sqrt(fan_in)
            k1, k2 = jax.random.split(k)
            W = jax.random.uniform(k1, (fan_in, fan_out), jnp.float32, -bound, bound)
            b = jax.random.uniform(k2, (fan_out,), jnp.float32, -bound, bound)
            return (W, b)
        Wq, bq = lin(ks[0], D, D)
        Wk, bk = lin(ks[1], D, D)
        Wv, bv = lin(ks[2], D, D)
        W1, b1 = lin(ks[3], D, 4 * D)
        W2, b2 = lin(ks[4], 4 * D, D)
        Wc, bc = lin(ks[5], 2 * D, 6 * D)
        return {'x': jax.random.normal(ks[6], (B, S, D), jnp.float32), 't': jax.random.normal(ks[7], (B, D), jnp.float32), 'c': jax.random.normal(ks[8], (B, D), jnp.float32), 'Wq': Wq, 'bq': bq, 'Wk': Wk, 'bk': bk, 'Wv': Wv, 'bv': bv, 'W1': W1, 'b1': b1, 'W2': W2, 'b2': b2, 'Wc': Wc, 'bc': bc, 'ln1_g': jnp.ones((D,), jnp.float32), 'ln1_b': jnp.zeros((D,), jnp.float32), 'ln2_g': jnp.ones((D,), jnp.float32), 'ln2_b': jnp.zeros((D,), jnp.float32)}
    _L0_cond_all = _L0_cond_setup()
    _L0_cond_in = {k: v for k, v in _L0_cond_all.items() if k in ('Wq', 'bq', 'Wk', 'bk', 'Wv', 'bv', 'W1', 'b1', 'W2', 'b2', 'Wc', 'bc', 'ln1_g', 'ln1_b', 'ln2_g', 'ln2_b')}
    del _L0_cond_all
    return {'x': x, 'fside_BxS_0': fside_BxS_0, 'cond_1024': cond_1024, 'L0_cond_Wq': _L0_cond_in['Wq'], 'L0_cond_bq': _L0_cond_in['bq'], 'L0_cond_Wk': _L0_cond_in['Wk'], 'L0_cond_bk': _L0_cond_in['bk'], 'L0_cond_Wv': _L0_cond_in['Wv'], 'L0_cond_bv': _L0_cond_in['bv'], 'L0_cond_W1': _L0_cond_in['W1'], 'L0_cond_b1': _L0_cond_in['b1'], 'L0_cond_W2': _L0_cond_in['W2'], 'L0_cond_b2': _L0_cond_in['b2'], 'L0_cond_Wc': _L0_cond_in['Wc'], 'L0_cond_bc': _L0_cond_in['bc'], 'L0_cond_ln1_g': _L0_cond_in['ln1_g'], 'L0_cond_ln1_b': _L0_cond_in['ln1_b'], 'L0_cond_ln2_g': _L0_cond_in['ln2_g'], 'L0_cond_ln2_b': _L0_cond_in['ln2_b']}

def reference(x, fside_BxS_0, cond_1024, L0_cond_Wq, L0_cond_bq, L0_cond_Wk, L0_cond_bk, L0_cond_Wv, L0_cond_bv, L0_cond_W1, L0_cond_b1, L0_cond_W2, L0_cond_b2, L0_cond_Wc, L0_cond_bc, L0_cond_ln1_g, L0_cond_ln1_b, L0_cond_ln2_g, L0_cond_ln2_b):
    import jax
    import jax.numpy as jnp

    def _L0_cond_ref(x, t, c, Wq, bq, Wk, bk, Wv, bv, W1, b1, W2, b2, Wc, bc, ln1_g, ln1_b, ln2_g, ln2_b):
        import jax, jax.numpy as jnp
        import numpy as np
        B, S, D = (8, 128, 128)
        EPS = 1e-05

        def _layernorm(h, g, b):
            mu = jnp.mean(h, axis=-1, keepdims=True)
            var = jnp.mean((h - mu) ** 2, axis=-1, keepdims=True)
            return (h - mu) * jax.lax.rsqrt(var + EPS) * g + b
        dim = x.shape[-1]
        cond = jnp.concatenate([t, c], axis=-1) @ Wc + bc
        a1, g1, be1, a2, g2, be2 = jnp.split(cond[:, None, :], 6, axis=-1)
        h = _layernorm(x, ln1_g, ln1_b) * (1.0 + g1) + be1
        Q = h @ Wq + bq
        K = h @ Wk + bk
        V = h @ Wv + bv
        scores = jnp.einsum('bsd,btd->bst', Q, K) / jnp.sqrt(jnp.float32(dim))
        attn = jax.nn.softmax(scores, axis=-1) @ V
        x = x + a1 * attn
        h = _layernorm(x, ln2_g, ln2_b) * (1.0 + g2) + be2
        h = jax.nn.gelu(h @ W1 + b1, approximate=False)
        h = jax.nn.gelu(h @ W2 + b2, approximate=False)
        x = x + a2 * h
        return x
    x = _L0_cond_ref(x, fside_BxS_0, cond_1024, L0_cond_Wq, L0_cond_bq, L0_cond_Wk, L0_cond_bk, L0_cond_Wv, L0_cond_bv, L0_cond_W1, L0_cond_b1, L0_cond_W2, L0_cond_b2, L0_cond_Wc, L0_cond_bc, L0_cond_ln1_g, L0_cond_ln1_b, L0_cond_ln2_g, L0_cond_ln2_b)
    return x

_drawn_inputs = setup_inputs


def setup_inputs(seed=0):
    import zlib

    import numpy as np

    out = dict(_drawn_inputs(seed))
    spreads = {'L0_cond_ln1_g': (1.0, 0.6),
     'L0_cond_ln1_b': (0.0, 0.1),
     'L0_cond_ln2_g': (1.0, 0.6),
     'L0_cond_ln2_b': (0.0, 0.8)}
    factors = {'L0_cond_bq': 8.0,
     'L0_cond_bk': 8.0,
     'L0_cond_b1': 8.0,
     'L0_cond_b2': 7.281,
     'L0_cond_bc': 3.001}
    for name, (base, spread) in spreads.items():
        noise = np.random.default_rng([zlib.crc32(name.encode()), seed]).standard_normal(out[name].shape)
        drawn = base * np.exp(spread * noise) if base else spread * noise
        out[name] = jnp.asarray(drawn.astype(out[name].dtype))
    for name, factor in factors.items():
        out[name] = (out[name] * factor).astype(out[name].dtype)
    return out
```

```python
from contextlib import ExitStack

import concourse.bass as bass
from concourse import mybir

F32 = mybir.dt.float32
F32R = mybir.dt.float32r
ALU = mybir.AluOpType
ACT = mybir.ActivationFunctionType
AX_X = mybir.AxisListType.X
ds = bass.ds

P = 128
GB = 4
GW = GB * P
EPS = 1e-5
LOOP_FROM = 2
LOOP_PAIRS = 2


def cond_block_kernel(nc, x, t, c, Wq, bq, Wk, bk, Wv, bv, W1, b1, W2, b2, Wc, bc,
                      ln1_g, ln1_b, ln2_g, ln2_b, out):
    B, S, D = x.shape
    assert S == P and D == P and B % GB == 0
    G = B // GB
    HC = W1.shape[1] // P
    KC = Wc.shape[0] // P
    MC = Wc.shape[1] // P
    SCALE = float(D) ** -0.5
    A1, G1, BE1, A2, G2, BE2 = range(MC)
    BQ, BK, B2, LG1, LB1, LG2, LB2 = range(7)
    B1 = 7
    BC = B1 + HC
    NV = BC + MC

    def inside(g):
        return 0 <= g < G if isinstance(g, int) else True

    def steps(eng, step, first, last):
        after = LOOP_FROM + 2 * LOOP_PAIRS
        for i in range(first, LOOP_FROM):
            step(i, i % 2)
        with eng.Fori(0, LOOP_PAIRS) as r:
            for u in range(2):
                step(2 * r + (LOOP_FROM + u), (LOOP_FROM + u) % 2)
        for i in range(after, last + 1):
            step(i, i % 2)

    def reuse(eng, semaphore, value):
        if not isinstance(value, int) or value > 0:
            eng.wait_ge(semaphore, value)

    with ExitStack() as ctx:
        def sb(name, shape, dt=F32):
            return ctx.enter_context(nc.sbuf_tensor(name, shape, dt))

        def sem(name):
            return ctx.enter_context(nc.semaphore(name))

        x_all = sb("x_all", [P, G * GW])
        x1_all = sb("x1_all", [P, G * GW])
        gate1 = sb("gate1", [P, G, 2, GW])
        ident = sb("ident", [P, P])
        wq, wk, wv = (sb(n, [P, P]) for n in ("wq", "wk", "wv"))
        w1 = sb("w1", [P, HC * P])
        w2 = sb("w2", [P, HC, P])
        w1_hi, w1_lo = (sb(n, [P, HC * P], F32R) for n in ("w1_hi", "w1_lo"))
        w2_hi, w2_lo = (sb(n, [P, HC, P], F32R) for n in ("w2_hi", "w2_lo"))
        wc = sb("wc", [P, KC, MC * P])
        vec_rows = sb("vec_rows", [NV, P])
        vec = sb("vec", [P, NV])
        bq_scaled = sb("bq_scaled", [P, 1])
        tc_rows = sb("tc_rows", [B, KC, P])
        tc_T = sb("tc_T", [P, KC, B])
        bc_row, bv_row = (sb(n, [B, P]) for n in ("bc_row", "bv_row"))
        gate_rows = sb("gate_rows", [B, 2, P])
        one_g = sb("one_g", [P, 2, B])
        shift_part = sb("shift_part", [P, 2, B])
        scale1, shift1, scale2, shift2, a2 = (
            sb(n, [P, B]) for n in ("scale1", "shift1", "scale2", "shift2", "a2"))
        eps = sb("eps", [P, GB])
        minus_half = sb("minus_half", [P, GB])
        stats = sb("stats", [P, 2, GB, 6])
        moments = sb("moments", [P, 2, GB, 2])
        var_eps = sb("var_eps", [P, 2, GB])
        rstd = sb("rstd", [P, 2, GB])
        n_tok = sb("n_tok", [P, 2, GW])
        hT = sb("hT", [P, 2, GW])
        qT = sb("qT", [P, 2, GW])
        kT = sb("kT", [P, 2, GW])
        v_gated = sb("v_gated", [P, 2, GW])
        neg_max = sb("neg_max", [P, 2, GB])
        probs = sb("probs", [P, 2, GW])
        row_sum = sb("row_sum", [P, 2, GB])
        inv_sum = sb("inv_sum", [P, 2, GB])
        pT = sb("pT", [P, 2, GW])
        x_bias = sb("x_bias", [P, 2, GW])
        out_tok = sb("out_tok", [P, 2, GW])
        h2 = sb("h2", [P, GW])
        h2_hi, h2_lo = (sb(n, [P, GW], F32R) for n in ("h2_hi", "h2_lo"))
        act1 = sb("act1", [P, HC, GW])
        act1_hi, act1_lo = (sb(n, [P, HC, GW], F32R) for n in ("act1_hi", "act1_lo"))
        act2 = sb("act2", [P, GW])
        act2_gated = sb("act2_gated", [P, GW])
        gate_dram = nc.dram_tensor("gate_dram", [2, B, P], F32, kind="Internal").ap()

        bank = [ctx.enter_context(nc.psum_tensor(f"bank{i}", [P, GW], F32)) for i in range(8)]
        ps_nT, ps_q, ps_k, ps_v, ps_s, ps_pT, ps_o, ps_vec = bank
        ps_hid = [bank[1], bank[2], bank[3], bank[7]]
        ps_y, ps_oT = ps_s, ps_pT
        ps_tc, ps_cond, ps_gate = ps_o, ps_pT, ps_s

        x_in = [sem("x_in0"), sem("x_in1")]
        gate_in = [sem("gate_in0"), sem("gate_in1")]
        vec_in, tc_in, wc_in, qkv_in, rows_in, w1_in, w2_in = (
            sem(n) for n in ("vec_in", "tc_in", "wc_in", "qkv_in", "rows_in", "w1_in", "w2_in"))
        zeroed, consts_ready = sem("zeroed"), sem("consts_ready")
        vec_T, tc_done, cond_done, gate_done = (
            sem(n) for n in ("vec_T", "tc_done", "cond_done", "gate_done"))
        vec_ready, tc_ready, setup_step, mod_ready, gate_row, gate_rows_ready, gate_stored = (
            sem(n) for n in ("vec_ready", "tc_ready", "setup_step", "mod_ready", "gate_row",
                             "gate_rows_ready", "gate_stored"))
        w1_hi_ready, w2_hi_ready, w_split = sem("w1_hi_ready"), sem("w2_hi_ready"), sem("w_split")
        stats_done, moments_ready, var_ready, rstd_ready, n_ready, nT_ready = (
            sem(n) for n in ("stats_done", "moments_ready", "var_ready", "rstd_ready", "n_ready",
                             "nT_ready"))
        hT_ready, q_done, k_done, v_done, qT_ready, kT_ready, v_ready = (
            sem(n) for n in ("hT_ready", "q_done", "k_done", "v_done", "qT_ready", "kT_ready",
                             "v_ready"))
        scores_done, max_ready, probs_ready, pT_done, pT_ready, o_done = (
            sem(n) for n in ("scores_done", "max_ready", "probs_ready", "pT_done", "pT_ready",
                             "o_done"))
        x_bias_ready, inv_ready, x1_ready = (
            sem(n) for n in ("x_bias_ready", "inv_ready", "x1_ready"))
        h2_ready, h2_hi_ready, h2_split = (
            sem(n) for n in ("h2_ready", "h2_hi_ready", "h2_split"))
        hid_done, act1_ready, act1_hi_ready = (
            sem(n) for n in ("hid_done", "act1_ready", "act1_hi_ready"))
        act1_lo_pool, act1_lo_dve = sem("act1_lo_pool"), sem("act1_lo_dve")
        y_done, act2_ready, gated_ready, oT_done, out_ready = (
            sem(n) for n in ("y_done", "act2_ready", "gated_ready", "oT_done", "out_ready"))
        stored = [sem("stored0"), sem("stored1")]

        def col(i):
            return vec[:, i:i + 1]

        def seq(b):
            return slice(b * P, (b + 1) * P)

        def dma_count(g, p):
            return 8 * (g - p) + 16

        block = ctx.enter_context(nc.Block())

        @block.sync
        def _(sp):
            def load_x(g, p):
                sp.dma_start(x_all[:, ds(g * GW, GW)].rearrange("s (b d) -> s b d", b=GB),
                             x[ds(g * GB, GB)].rearrange("b s d -> s b d")).then_inc(x_in[p], 16)

            def load_gate(g, p):
                sp.dma_start(gate1[:, ds(g, 1), :, :].rearrange("s a k n -> s (a k) n"),
                             gate_dram[:, ds(g * GB, GB), :].rearrange("k b d -> k (b d)")
                             .partition_broadcast(P)).then_inc(gate_in[p], 16)

            for u in range(2):
                sp.sem_inc(stored[u], 16)
            load_x(0, 0)
            for i, row in enumerate((bq, bk, b2, ln1_g, ln1_b, ln2_g, ln2_b)):
                sp.dma_start(vec_rows[i:i + 1, :], row.rearrange("(a d) -> a d", a=1)).then_inc(vec_in, 16)
            sp.dma_start(vec_rows[B1:B1 + HC, :], b1.rearrange("(a d) -> a d", d=P)).then_inc(vec_in, 16)
            sp.dma_start(vec_rows[BC:BC + MC, :], bc.rearrange("(a d) -> a d", d=P)).then_inc(vec_in, 16)
            load_x(1, 1)
            sp.wait_ge(gate_rows_ready, 1)
            sp.dma_start(gate_dram.rearrange("k b d -> b k d"), gate_rows[:]).then_inc(gate_stored, 16)
            sp.wait_ge(gate_stored, 16)
            load_gate(0, 0)
            load_gate(1, 1)
            sp.dma_start(w1[:], W1).then_inc(w1_in, 16)
            sp.dma_start(w2[:], W2.rearrange("(k p) d -> p k d", p=P)).then_inc(w2_in, 16)
            with sp.Fori(0, G // 2 - 1) as r:
                for u in range(2):
                    g = 2 * r + (2 + u)
                    sp.wait_ge(x_in[u], dma_count(g - 2, u))
                    load_x(g, u)
                    sp.wait_ge(gate_in[u], dma_count(g - 2, u))
                    load_gate(g, u)
            with sp.Fori(0, G // 2) as r:
                for u in range(2):
                    g = 2 * r + u
                    sp.wait_ge(out_ready, g + 1)
                    sp.dma_start(out[ds(g * GB, GB)].rearrange("b s d -> s b d"),
                                 out_tok[:, u, :].rearrange("s (b d) -> s b d", b=GB)).then_inc(stored[u], 16)
            for u in range(2):
                sp.wait_ge(stored[u], 16 * (G // 2 + 1))

        @block.gpsimd
        def _(pool):
            pool.memset(ident[:], 0.0).then_inc(zeroed, 1)
            pool.memset(eps[:], EPS)
            pool.memset(minus_half[:], -0.5)
            pool.wait_ge(zeroed, 1)
            pool.affine_select(out=ident[:], in_=ident[:], compare_op=ALU.not_equal, fill=1.0, base=0,
                               pattern=[[-1, P]], channel_multiplier=1).then_inc(consts_ready, 1)

            def rsqrt(k, p):
                pool.wait_ge(moments_ready, k + 1)
                pool.tensor_tensor(var_eps[:, p, :], moments[:, p, :, 1], eps[:], ALU.add).then_inc(var_ready, 1)
                pool.wait_ge(var_ready, k + 1)
                pool.tensor_tensor(rstd[:, p, :], var_eps[:, p, :], minus_half[:], ALU.pow).then_inc(rstd_ready, 1)

            def residual_bias(g, p):
                pool.wait_ge(x_in[p], dma_count(g, p))
                pool.wait_ge(gate_in[p], dma_count(g, p))
                reuse(pool, x1_ready, g - 1)
                pool.tensor_tensor(x_bias[:, p, :], x_all[:, ds(g * GW, GW)],
                                   gate1[:, ds(g, 1), 1, :].rearrange("s a n -> s (a n)"),
                                   ALU.add).then_inc(x_bias_ready, 1)

            def phase_a(i, p):
                if inside(i + 2):
                    rsqrt(i + 2, p)
                if inside(i):
                    residual_bias(i, p)
                if isinstance(i, int) and i == 0:
                    pool.wait_ge(w1_hi_ready, 1)
                    pool.tensor_tensor(w1_lo[:], w1[:], w1_hi[:].bitcast(F32), ALU.subtract).then_inc(w_split, 1)
                    pool.wait_ge(w2_hi_ready, 1)
                    pool.tensor_tensor(w2_lo[:], w2[:], w2_hi[:].bitcast(F32), ALU.subtract).then_inc(w_split, 1)

            def phase_b(i, p):
                if inside(i + 2):
                    rsqrt(G + i + 2, p)
                if inside(i + 1):
                    for j in range(0, HC, 2):
                        pool.wait_ge(act1_hi_ready, HC * (i + 1) + j + 1)
                        pool.tensor_tensor(act1_lo[:, j, :], act1[:, j, :], act1_hi[:, j, :].bitcast(F32),
                                           ALU.subtract).then_inc(act1_lo_pool, 1)

            steps(pool, phase_a, -2, G - 1)
            steps(pool, phase_b, -2, G - 2)

        @block.scalar
        def _(act):
            act.dma_start(tc_rows[:, 0, :], t).then_inc(tc_in, 16)
            act.dma_start(tc_rows[:, 1, :], c).then_inc(tc_in, 16)
            act.dma_start(wc[:], Wc.rearrange("(k p) m -> p k m", p=P)).then_inc(wc_in, 16)
            for sb_w, dram_w in ((wq, Wq), (wk, Wk), (wv, Wv)):
                act.dma_start(sb_w[:], dram_w).then_inc(qkv_in, 16)
            act.dma_start(bc_row[:], bc[0:P].partition_broadcast(B)).then_inc(rows_in, 16)
            act.dma_start(bv_row[:], bv.partition_broadcast(B)).then_inc(rows_in, 16)

            def modulate(k, g, p, scale, shift, dest, done):
                act.wait_ge(nT_ready, k + 1)
                for b in range(GB):
                    last = act.activation(dest[:, seq(b)], ps_nT[:, seq(b)], ACT.Identity,
                                          bias=shift[:, ds(g * GB + b, 1)], scale=scale[:, ds(g * GB + b, 1)])
                last.then_inc(done, 1)

            def phase_a(i, p):
                q = 1 - p
                if inside(i + 1):
                    reuse(act, v_done, i)
                    modulate(i + 1, i + 1, q, scale1, shift1, hT[:, q, :], hT_ready)
                if inside(i):
                    act.wait_ge(max_ready, i + 1)
                    reuse(act, pT_done, i - 1)
                    reuse(act, inv_ready, i - 1)
                    for b in range(GB):
                        last = act.activation(probs[:, p, seq(b)], ps_s[:, seq(b)], ACT.Exp,
                                              bias=neg_max[:, p, b:b + 1],
                                              accum_out=row_sum[:, p, b:b + 1])
                    last.then_inc(probs_ready, 1)
                if inside(i + 1):
                    act.wait_ge(q_done, i + 2)
                    reuse(act, scores_done, i)
                    act.activation(qT[:, q, :], ps_q[:], ACT.Identity, bias=bq_scaled[:],
                                   scale=SCALE).then_inc(qT_ready, 1)
                    act.wait_ge(k_done, i + 2)
                    act.activation(kT[:, q, :], ps_k[:], ACT.Identity, bias=col(BK)).then_inc(kT_ready, 1)
                if inside(i):
                    act.wait_ge(pT_done, i + 1)
                    reuse(act, o_done, i - 1)
                    act.activation(pT[:, p, :], ps_pT[:], ACT.Copy).then_inc(pT_ready, 1)
                if isinstance(i, int) and i == 0:
                    act.wait_ge(w1_in, 16)
                    act.activation(w1_hi[:], w1[:], ACT.Copy).then_inc(w1_hi_ready, 1)
                    act.wait_ge(w2_in, 16)
                    act.activation(w2_hi[:], w2[:], ACT.Copy).then_inc(w2_hi_ready, 1)

            def phase_b(i, p):
                if inside(i + 1):
                    modulate(G + i + 1, i + 1, p, scale2, shift2, h2, h2_ready)
                if inside(i):
                    act.wait_ge(y_done, i + 1)
                    act.activation(act2[:], ps_y[:], ACT.Gelu, bias=col(B2)).then_inc(act2_ready, 1)
                    act.wait_ge(act2_ready, i + 1)
                    for b in range(GB):
                        last = act.activation(act2_gated[:, seq(b)], act2[:, seq(b)], ACT.Copy,
                                              scale=a2[:, ds(i * GB + b, 1)])
                    last.then_inc(gated_ready, 1)
                if inside(i + 1):
                    for j in range(HC):
                        act.wait_ge(hid_done, HC * (i + 1) + j + 1)
                        act.activation(act1[:, j, :], ps_hid[j][:], ACT.Gelu,
                                       bias=col(B1 + j)).then_inc(act1_ready, 1)

            act.wait_ge(mod_ready, 2)
            act.wait_ge(vec_ready, 2)
            steps(act, phase_a, -1, G - 1)
            act.wait_ge(mod_ready, 5)
            steps(act, phase_b, -1, G - 1)

        @block.vector
        def _(dve):
            def layernorm_stats(k, src, g, p, between=None):
                for b in range(GB):
                    last = dve.bn_stats(stats[:, p, b, :], src[:, ds(g * GW + b * P, P)])
                last.then_inc(stats_done, 1)
                dve.wait_ge(stats_done, k + 1)
                if between:
                    between()
                for b in range(GB):
                    last = dve.bn_aggr(moments[:, p, b, :], stats[:, p, b, :])
                last.then_inc(moments_ready, 1)

            def normalize(k, src, g, p):
                dve.wait_ge(rstd_ready, k + 1)
                reuse(dve, nT_ready, k - 1)
                for b in range(GB):
                    last = dve.tensor_scalar(n_tok[:, p, seq(b)], src[:, ds(g * GW + b * P, P)],
                                             moments[:, p, b, 0:1], rstd[:, p, b:b + 1],
                                             ALU.subtract, ALU.mult)
                last.then_inc(n_ready, 1)

            def stats_a(g, p, between=None):
                dve.wait_ge(x_in[p], dma_count(g, p))
                layernorm_stats(g, x_all, g, p, between)

            def phase_a(i, p):
                q = 1 - p
                if inside(i):
                    dve.wait_ge(scores_done, i + 1)
                    reuse(dve, probs_ready, i - 1)
                    dve.tensor_reduce(neg_max[:, p, :], ps_s[:].rearrange("s (b t) -> s b t", b=GB),
                                      AX_X, ALU.max, negate=True).then_inc(max_ready, 1)

                def invert_sums():
                    if inside(i - 1):
                        dve.wait_ge(probs_ready, i)
                        dve.reciprocal(inv_sum[:, q, :], row_sum[:, q, :]).then_inc(inv_ready, 1)

                if inside(i + 2):
                    stats_a(i + 2, p, invert_sums)
                else:
                    invert_sums()
                if inside(i - 1):
                    dve.wait_ge(inv_ready, i)
                    dve.wait_ge(x_bias_ready, i)
                    dve.wait_ge(o_done, i)
                    for b in range(GB):
                        last = dve.scalar_tensor_tensor(x1_all[:, ds((i - 1) * GW + b * P, P)],
                                                        ps_o[:, seq(b)], inv_sum[:, q, b:b + 1],
                                                        x_bias[:, q, seq(b)], ALU.mult, ALU.add)
                    last.then_inc(x1_ready, 1)
                if inside(i + 2):
                    normalize(i + 2, x_all, i + 2, p)
                if inside(i + 1):
                    dve.wait_ge(v_done, i + 2)
                    dve.wait_ge(gate_in[q], dma_count(i + 1, q))
                    reuse(dve, o_done, i)
                    dve.tensor_tensor(v_gated[:, q, :], ps_v[:],
                                      gate1[:, ds(i + 1, 1), 0, :].rearrange("s a n -> s (a n)"),
                                      ALU.mult).then_inc(v_ready, 1)

            def phase_b(i, p):
                q = 1 - p
                if inside(i - 1):
                    dve.wait_ge(oT_done, i)
                    dve.wait_ge(stored[q], dma_count(i - 1, q))
                    dve.tensor_tensor(out_tok[:, q, :], ps_oT[:], x1_all[:, ds((i - 1) * GW, GW)],
                                      ALU.add).then_inc(out_ready, 1)

                def h2_high():
                    if inside(i + 1):
                        dve.wait_ge(h2_ready, i + 2)
                        dve.tensor_copy(h2_hi[:], h2[:]).then_inc(h2_hi_ready, 1)

                if inside(i + 2):
                    dve.wait_ge(x1_ready, i + 3)
                    layernorm_stats(G + i + 2, x1_all, i + 2, p, h2_high)
                else:
                    h2_high()
                if inside(i + 1):
                    dve.wait_ge(h2_hi_ready, i + 2)
                    dve.tensor_tensor(h2_lo[:], h2[:], h2_hi[:].bitcast(F32), ALU.subtract)\
                        .then_inc(h2_split, 1)
                for j in range(HC):
                    if inside(i + 1):
                        dve.wait_ge(act1_ready, HC * (i + 1) + j + 1)
                        dve.tensor_copy(act1_hi[:, j, :], act1[:, j, :]).then_inc(act1_hi_ready, 1)
                        if j % 2:
                            dve.wait_ge(act1_hi_ready, HC * (i + 1) + j + 1)
                            dve.tensor_tensor(act1_lo[:, j, :], act1[:, j, :], act1_hi[:, j, :].bitcast(F32),
                                              ALU.subtract).then_inc(act1_lo_dve, 1)
                    if inside(i + 2) and j == 0:
                        normalize(G + i + 2, x1_all, i + 2, p)

            dve.wait_ge(vec_T, 1)
            dve.tensor_copy(vec[:], ps_vec[:, 0:NV]).then_inc(vec_ready, 1)
            dve.wait_ge(tc_done, 1)
            dve.tensor_copy(tc_T[:].rearrange("p k b -> p (k b)"), ps_tc[:, 0:KC * B]).then_inc(tc_ready, 1)
            dve.wait_ge(vec_ready, 1)
            dve.tensor_scalar(bq_scaled[:], col(BQ), SCALE, None, ALU.mult).then_inc(vec_ready, 1)
            stats_a(0, 0)

            def cond(m):
                return ps_cond[:, m * B:(m + 1) * B]

            dve.wait_ge(cond_done, 1)
            for n, g_out in enumerate((G1, G2)):
                dve.tensor_scalar(one_g[:, n, :], cond(g_out), col(BC + g_out), 1.0, ALU.add,
                                  ALU.add).then_inc(setup_step, 1)
            dve.wait_ge(setup_step, 2)
            dve.tensor_scalar(scale1[:], one_g[:, 0, :], col(LG1), None, ALU.mult).then_inc(mod_ready, 1)
            dve.tensor_scalar(shift_part[:, 0, :], one_g[:, 0, :], col(LB1), col(BC + BE1), ALU.mult,
                              ALU.add)
            dve.tensor_scalar(shift_part[:, 1, :], one_g[:, 1, :], col(LB2), col(BC + BE2), ALU.mult,
                              ALU.add).then_inc(setup_step, 1)
            dve.wait_ge(setup_step, 3)
            dve.tensor_tensor(shift1[:], cond(BE1), shift_part[:, 0, :], ALU.add).then_inc(mod_ready, 1)
            normalize(0, x_all, 0, 0)
            dve.wait_ge(gate_done, 1)
            dve.wait_ge(rows_in, 32)
            dve.tensor_tensor(gate_rows[:, 0, :], ps_gate[0:B, 0:P], bc_row[:], ALU.add).then_inc(gate_row, 1)
            dve.wait_ge(gate_row, 1)
            dve.tensor_tensor(gate_rows[:, 1, :], gate_rows[:, 0, :], bv_row[:], ALU.mult)\
                .then_inc(gate_rows_ready, 1)
            dve.tensor_scalar(scale2[:], one_g[:, 1, :], col(LG2), None, ALU.mult).then_inc(mod_ready, 1)
            dve.tensor_tensor(shift2[:], cond(BE2), shift_part[:, 1, :], ALU.add).then_inc(mod_ready, 1)
            dve.tensor_scalar(a2[:], cond(A2), col(BC + A2), None, ALU.add).then_inc(mod_ready, 1)
            steps(dve, phase_a, -1, G)
            steps(dve, phase_b, -2, G)

        @block.tensor
        def _(pe):
            def transpose_group(dest, src, done):
                for b in range(GB):
                    last = pe.transpose(dest[:, seq(b)], src[:, seq(b)], ident[:])
                last.then_inc(done, 1)

            def split_product(dest, w_hi, w_lo, m_hi, m_lo, start, stop):
                pe.matmul(dest, w_lo, m_hi, start=start, stop=False)
                pe.matmul(dest, w_hi, m_hi, start=False, stop=False)
                return pe.matmul(dest, w_hi, m_lo, start=False, stop=stop)

            def phase_a(i, p):
                q = 1 - p
                if inside(i + 1):
                    pe.wait_ge(n_ready, i + 2)
                    transpose_group(ps_nT, n_tok[:, q, :], nT_ready)
                if inside(i):
                    pe.wait_ge(qT_ready, i + 1)
                    pe.wait_ge(kT_ready, i + 1)
                    reuse(pe, probs_ready, i)
                    for b in range(GB):
                        last = pe.matmul(ps_s[:, seq(b)], qT[:, p, seq(b)], kT[:, p, seq(b)],
                                         start=True, stop=True)
                    last.then_inc(scores_done, 1)
                if inside(i - 1):
                    pe.wait_ge(pT_ready, i)
                    pe.wait_ge(v_ready, i)
                    reuse(pe, x1_ready, i - 1)
                    for b in range(GB):
                        last = pe.matmul(ps_o[:, seq(b)], pT[:, q, seq(b)], v_gated[:, q, seq(b)],
                                         start=True, stop=True)
                    last.then_inc(o_done, 1)
                if inside(i + 1):
                    pe.wait_ge(hT_ready, i + 2)
                    reuse(pe, qT_ready, i + 1)
                    pe.matmul(ps_q[:], wq[:], hT[:, q, :], start=True, stop=True).then_inc(q_done, 1)
                    reuse(pe, kT_ready, i + 1)
                    pe.matmul(ps_k[:], wk[:], hT[:, q, :], start=True, stop=True).then_inc(k_done, 1)
                    reuse(pe, v_ready, i + 1)
                    for b in range(GB):
                        last = pe.matmul(ps_v[:, seq(b)], hT[:, q, seq(b)], wv[:], start=True, stop=True)
                    last.then_inc(v_done, 1)
                if inside(i):
                    pe.wait_ge(probs_ready, i + 1)
                    reuse(pe, pT_ready, i)
                    transpose_group(ps_pT, probs[:, p, :], pT_done)

            def phase_b(i, p):
                if inside(i + 1):
                    pe.wait_ge(n_ready, G + i + 2)
                    transpose_group(ps_nT, n_tok[:, 1 - p, :], nT_ready)
                if inside(i - 1):
                    pe.wait_ge(gated_ready, i)
                    reuse(pe, out_ready, i - 1)
                    transpose_group(ps_oT, act2_gated, oT_done)
                if inside(i):
                    for j in range(HC):
                        pe.wait_ge(act1_hi_ready, HC * i + j + 1)
                        if j % 2:
                            pe.wait_ge(act1_lo_dve, HC // 2 * i + j // 2 + 1)
                        else:
                            pe.wait_ge(act1_lo_pool, HC // 2 * i + j // 2 + 1)
                        last = split_product(ps_y[:], w2_hi[:, j, :], w2_lo[:, j, :], act1_hi[:, j, :],
                                             act1_lo[:, j, :], start=j == 0, stop=j == HC - 1)
                    last.then_inc(y_done, 1)
                if inside(i + 1):
                    pe.wait_ge(h2_split, i + 2)
                    for j in range(HC):
                        split_product(ps_hid[j][:], w1_hi[:, seq(j)], w1_lo[:, seq(j)], h2_hi[:],
                                      h2_lo[:], start=True, stop=True).then_inc(hid_done, 1)

            pe.wait_ge(consts_ready, 1)
            pe.wait_ge(tc_in, 32)
            for k in range(KC):
                last = pe.transpose(ps_tc[:, k * B:(k + 1) * B], tc_rows[:, k, :], ident[0:B, 0:B])
            last.then_inc(tc_done, 1)
            pe.wait_ge(vec_in, 16 * 9)
            pe.transpose(ps_vec[:, 0:NV], vec_rows[:], ident[0:NV, 0:NV]).then_inc(vec_T, 1)
            pe.wait_ge(tc_ready, 1)
            pe.wait_ge(wc_in, 16)
            for m in (G1, BE1, A2, G2, BE2):
                for k in range(KC):
                    last = pe.matmul(ps_cond[:, m * B:(m + 1) * B], wc[:, k, seq(m)], tc_T[:, k, :],
                                     start=k == 0, stop=k == KC - 1)
            last.then_inc(cond_done, 1)
            for k in range(KC):
                last = pe.matmul(ps_gate[0:B, 0:P], tc_T[:, k, :], wc[:, k, seq(A1)],
                                 start=k == 0, stop=k == KC - 1)
            last.then_inc(gate_done, 1)
            pe.wait_ge(qkv_in, 48)
            steps(pe, phase_a, -1, G)
            pe.wait_ge(w_split, 2)
            steps(pe, phase_b, -1, G)


_INS = ["x", "fside_BxS_0", "cond_1024"] + [
    "L0_cond_" + n for n in ("Wq", "bq", "Wk", "bk", "Wv", "bv", "W1", "b1", "W2", "b2", "Wc", "bc",
                             "ln1_g", "ln1_b", "ln2_g", "ln2_b")]


def kernel(**inputs):
    import numpy as _np
    import concourse.bacc as _bacc
    from concourse import mybir as _mybir
    from concourse.bass_utils import run_bass_kernel_spmd as _run

    nc = _bacc.Bacc("TRN2", target_bir_lowering=False, num_devices=1)
    arrays, args = {}, []
    for name in _INS:
        a = _np.ascontiguousarray(inputs[name])
        arrays[f"in_{name}"] = a
        args.append(nc.dram_tensor(f"in_{name}", a.shape, _mybir.dt.from_np(a.dtype), kind="ExternalInput").ap())
    out = nc.dram_tensor("out_x", arrays["in_x"].shape, _mybir.dt.float32, kind="ExternalOutput").ap()
    cond_block_kernel(nc, *args, out)
    r = _run(nc, [arrays], core_ids=[0])
    return r.results[0]["out_x"]
```

```python
from contextlib import ExitStack

import concourse.bass as bass
from concourse import mybir

F32 = mybir.dt.float32
F32R = mybir.dt.float32r
ALU = mybir.AluOpType
ACT = mybir.ActivationFunctionType
AX_X = mybir.AxisListType.X
ds = bass.ds

P = 128
GB = 4
GW = GB * P
EPS = 1e-5
LOOP_FROM = 2
LOOP_PAIRS = 2


def cond_block_kernel(nc, x, t, c, Wq, bq, Wk, bk, Wv, bv, W1, b1, W2, b2, Wc, bc,
                      ln1_g, ln1_b, ln2_g, ln2_b, out):
    B, S, D = x.shape
    assert S == P and D == P and B % GB == 0
    G = B // GB
    HC = W1.shape[1] // P
    KC = Wc.shape[0] // P
    MC = Wc.shape[1] // P
    SCALE = float(D) ** -0.5
    A1, G1, BE1, A2, G2, BE2 = range(MC)
    BQ, BK, LG1, LB1, BC = range(5)
    NA = BC + MC
    B2, LG2, LB2, B1 = range(4)
    NB = B1 + HC

    def inside(g):
        return 0 <= g < G if isinstance(g, int) else True

    def steps(eng, step, first, last):
        after = LOOP_FROM + 2 * LOOP_PAIRS
        for i in range(first, LOOP_FROM):
            step(i, i % 2)
        with eng.Fori(0, LOOP_PAIRS) as r:
            for u in range(2):
                step(2 * r + (LOOP_FROM + u), (LOOP_FROM + u) % 2)
        for i in range(after, last + 1):
            step(i, i % 2)

    def reuse(eng, semaphore, value):
        if not isinstance(value, int) or value > 0:
            eng.wait_ge(semaphore, value)

    with ExitStack() as ctx:
        def sb(name, shape, dt=F32):
            return ctx.enter_context(nc.sbuf_tensor(name, shape, dt))

        def sem(name):
            return ctx.enter_context(nc.semaphore(name))

        x_all = sb("x_all", [P, G * GW])
        x1_all = sb("x1_all", [P, G * GW])
        gate1 = sb("gate1", [P, G, 2, GW])
        ident = sb("ident", [P, P])
        wq, wk, wv = (sb(n, [P, P]) for n in ("wq", "wk", "wv"))
        w1 = sb("w1", [P, HC * P])
        w2 = sb("w2", [P, HC, P])
        w1_hi, w1_lo = (sb(n, [P, HC * P], F32R) for n in ("w1_hi", "w1_lo"))
        w2_hi, w2_lo = (sb(n, [P, HC, P], F32R) for n in ("w2_hi", "w2_lo"))
        wc = sb("wc", [P, KC, MC * P])
        rows_a, rows_b = sb("rows_a", [NA, P]), sb("rows_b", [NB, P])
        cols_a, cols_b = sb("cols_a", [P, NA]), sb("cols_b", [P, NB])
        bq_scaled = sb("bq_scaled", [P, 1])
        tc_rows = sb("tc_rows", [B, KC, P])
        tc_T = sb("tc_T", [P, KC, B])
        bc_row, bv_row = (sb(n, [B, P]) for n in ("bc_row", "bv_row"))
        gate_rows = sb("gate_rows", [B, 2, P])
        one_g = sb("one_g", [P, 2, B])
        shift_part = sb("shift_part", [P, 2, B])
        scale1, shift1, scale2, shift2, a2 = (
            sb(n, [P, B]) for n in ("scale1", "shift1", "scale2", "shift2", "a2"))
        mean2, rstd2 = sb("mean2", [P, B]), sb("rstd2", [P, B])
        eps = sb("eps", [P, GB])
        minus_half = sb("minus_half", [P, GB])
        stats, stats2 = (sb(n, [P, 2, GB, 6]) for n in ("stats", "stats2"))
        moments, moments2 = (sb(n, [P, 2, GB, 2]) for n in ("moments", "moments2"))
        var_eps, var_eps2 = (sb(n, [P, 2, GB]) for n in ("var_eps", "var_eps2"))
        wv_gated = sb("wv_gated", [P, 2, GW])
        n2_tok = sb("n2_tok", [P, 2, GW])
        rstd = sb("rstd", [P, 2, GB])
        n_tok = sb("n_tok", [P, 2, GW])
        hT = sb("hT", [P, 2, GW])
        qT = sb("qT", [P, 2, GW])
        kT = sb("kT", [P, 2, GW])
        v_tok = sb("v_tok", [P, 2, GW])
        neg_max = sb("neg_max", [P, 2, GB])
        probs = sb("probs", [P, 2, GW])
        row_sum = sb("row_sum", [P, 2, GB])
        inv_sum = sb("inv_sum", [P, 2, GB])
        pT = sb("pT", [P, 2, GW])
        x_bias = sb("x_bias", [P, 2, GW])
        act2 = sb("act2", [P, 2, GW])
        out_tok = sb("out_tok", [P, 2, GW])
        x1_centred = sb("x1_centred", [P, GW])
        h2 = sb("h2", [P, GW])
        h2_hi, h2_lo = (sb(n, [P, GW], F32R) for n in ("h2_hi", "h2_lo"))
        act1 = sb("act1", [P, HC, GW])
        act1_hi, act1_lo = (sb(n, [P, HC, GW], F32R) for n in ("act1_hi", "act1_lo"))
        act2_gated = sb("act2_gated", [P, GW])
        gate_dram = nc.dram_tensor("gate_dram", [2, B, P], F32, kind="Internal").ap()

        bank = [ctx.enter_context(nc.psum_tensor(f"bank{i}", [P, GW], F32)) for i in range(8)]
        ps_nT, ps_q, ps_k, ps_v, ps_s, ps_pT, ps_o, ps_vec = bank
        ps_n2T = ps_nT
        ps_hid = [bank[1], bank[2], bank[3], bank[7]]
        ps_y, ps_oT = ps_s, ps_pT
        ps_tc, ps_late, ps_cond1, ps_gate = ps_o, ps_o, ps_pT, ps_s

        x_in = [sem("x_in0"), sem("x_in1")]
        gate_in = [sem("gate_in0"), sem("gate_in1")]
        cols_a_in, cols_b_in, tc_in, qk_in, wv_in, bc_row_in, bv_row_in, w1_in, w2_in = (
            sem(n) for n in ("cols_a_in", "cols_b_in", "tc_in", "qk_in", "wv_in", "bc_row_in",
                             "bv_row_in", "w1_in", "w2_in"))
        wc_gate_in, wc_mod1_in, wc_rest_in = (
            sem(n) for n in ("wc_gate_in", "wc_mod1_in", "wc_rest_in"))
        zeroed, consts_ready = sem("zeroed"), sem("consts_ready")
        cols_a_T, tc_done, cond1_done, cond2_done, gate_done = (
            sem(n) for n in ("cols_a_T", "tc_done", "cond1_done", "cond2_done",
                             "gate_done"))
        cols_a_ready, cols_b_ready, tc_ready, bq_ready, mod1_step, mod1_ready, mod2_step, mod2_ready = (
            sem(n) for n in ("cols_a_ready", "cols_b_ready", "tc_ready", "bq_ready", "mod1_step",
                             "mod1_ready", "mod2_step", "mod2_ready"))
        gate_row, gate_rows_ready, gate_stored = (
            sem(n) for n in ("gate_row", "gate_rows_ready", "gate_stored"))
        w1_hi_ready, w2_hi_ready, w_split = sem("w1_hi_ready"), sem("w2_hi_ready"), sem("w_split")
        stats_done, moments_ready, var_ready, rstd_ready, n_ready, nT_ready = (
            sem(n) for n in ("stats_done", "moments_ready", "var_ready", "rstd_ready", "n_ready",
                             "nT_ready"))
        stats2_done, moments2_ready, var2_ready, rstd2_ready, centred, n2_ready, n2T_ready = (
            sem(n) for n in ("stats2_done", "moments2_ready", "var2_ready", "rstd2_ready", "centred",
                             "n2_ready", "n2T_ready"))
        wv_gated_ready = sem("wv_gated_ready")
        hT_ready, q_done, k_done, v_done, qT_ready, kT_ready, v_ready = (
            sem(n) for n in ("hT_ready", "q_done", "k_done", "v_done", "qT_ready", "kT_ready",
                             "v_ready"))
        scores_done, max_ready, probs_ready, pT_done, pT_ready, o_done = (
            sem(n) for n in ("scores_done", "max_ready", "probs_ready", "pT_done", "pT_ready",
                             "o_done"))
        x_bias_ready, inv_ready, x1_ready = (
            sem(n) for n in ("x_bias_ready", "inv_ready", "x1_ready"))
        h2_ready, h2_hi_ready, h2_split = (
            sem(n) for n in ("h2_ready", "h2_hi_ready", "h2_split"))
        hid_done, act1_ready, act1_hi_ready = (
            sem(n) for n in ("hid_done", "act1_ready", "act1_hi_ready"))
        act1_lo_pool, act1_lo_dve = sem("act1_lo_pool"), sem("act1_lo_dve")
        y_done, act2_ready, gated_ready, oT_done, out_ready = (
            sem(n) for n in ("y_done", "act2_ready", "gated_ready", "oT_done", "out_ready"))
        stored = [sem("stored0"), sem("stored1")]

        def col_a(i):
            return cols_a[:, i:i + 1]

        def col_b(i):
            return cols_b[:, i:i + 1]

        def seq(b):
            return slice(b * P, (b + 1) * P)

        def dma_count(g, p):
            return 8 * (g - p) + 16

        def cond(m):
            return (ps_cond1 if m in (G1, BE1) else ps_late)[:, m * B:(m + 1) * B]

        cols_b_at = MC * B

        block = ctx.enter_context(nc.Block())

        @block.sync
        def _(sp):
            def load_x(g, p):
                sp.dma_start(x_all[:, ds(g * GW, GW)].rearrange("s (b d) -> s b d", b=GB),
                             x[ds(g * GB, GB)].rearrange("b s d -> s b d")).then_inc(x_in[p], 16)

            def load_gate(g, p):
                sp.dma_start(gate1[:, ds(g, 1), :, :].rearrange("s a k n -> s (a k) n"),
                             gate_dram[:, ds(g * GB, GB), :].rearrange("k b d -> k (b d)")
                             .partition_broadcast(P)).then_inc(gate_in[p], 16)

            def row(v):
                return v.rearrange("(a d) -> a d", d=P)

            for u in range(2):
                sp.sem_inc(stored[u], 16)
            load_x(0, 0)
            sp.dma_start(bc_row[:], bc[0:P].partition_broadcast(B)).then_inc(bc_row_in, 16)
            sp.dma_start(rows_a[BC:BC + MC, :], row(bc)).then_inc(cols_a_in, 16)
            for i, v in ((LG1, ln1_g), (LB1, ln1_b), (BQ, bq), (BK, bk)):
                sp.dma_start(rows_a[i:i + 1, :], row(v)).then_inc(cols_a_in, 16)
            sp.dma_start(wv[:], Wv).then_inc(wv_in, 16)
            sp.wait_ge(gate_rows_ready, 1)
            sp.dma_start(gate_dram.rearrange("k b d -> b k d"), gate_rows[:]).then_inc(gate_stored, 16)
            load_x(1, 1)
            sp.wait_ge(gate_stored, 16)
            load_gate(0, 0)
            load_gate(1, 1)
            with sp.Fori(0, G // 2 - 1) as r:
                for u in range(2):
                    g = 2 * r + (2 + u)
                    sp.wait_ge(x_in[u], dma_count(g - 2, u))
                    load_x(g, u)
                    sp.wait_ge(gate_in[u], dma_count(g - 2, u))
                    load_gate(g, u)
            with sp.Fori(0, G // 2) as r:
                for u in range(2):
                    g = 2 * r + u
                    sp.wait_ge(out_ready, g + 1)
                    sp.dma_start(out[ds(g * GB, GB)].rearrange("b s d -> s b d"),
                                 out_tok[:, u, :].rearrange("s (b d) -> s b d", b=GB)).then_inc(stored[u], 16)
            for u in range(2):
                sp.wait_ge(stored[u], 16 * (G // 2 + 1))

        @block.gpsimd
        def _(pool):
            pool.memset(ident[:], 0.0).then_inc(zeroed, 1)
            pool.memset(eps[:], EPS)
            pool.memset(minus_half[:], -0.5)
            pool.wait_ge(zeroed, 1)
            pool.affine_select(out=ident[:], in_=ident[:], compare_op=ALU.not_equal, fill=1.0, base=0,
                               pattern=[[-1, P]], channel_multiplier=1).then_inc(consts_ready, 1)
            pool.dma_start(bv_row[:], bv.partition_broadcast(B)).then_inc(bv_row_in, 16)
            for i, v in ((B2, b2), (LG2, ln2_g), (LB2, ln2_b)):
                pool.dma_start(rows_b[i:i + 1, :], v.rearrange("(a d) -> a d", a=1)).then_inc(cols_b_in, 16)
            pool.dma_start(rows_b[B1:B1 + HC, :], b1.rearrange("(a d) -> a d", d=P)).then_inc(cols_b_in, 16)

            def rsqrt1(g, p):
                pool.wait_ge(moments_ready, g + 1)
                pool.tensor_tensor(var_eps[:, p, :], moments[:, p, :, 1], eps[:], ALU.add).then_inc(var_ready, 1)
                pool.wait_ge(var_ready, g + 1)
                pool.tensor_tensor(rstd[:, p, :], var_eps[:, p, :], minus_half[:], ALU.pow).then_inc(rstd_ready, 1)

            def rsqrt2(g, p):
                pool.wait_ge(moments2_ready, g + 1)
                pool.tensor_tensor(var_eps2[:, p, :], moments2[:, p, :, 1], eps[:], ALU.add).then_inc(var2_ready, 1)
                pool.tensor_copy(mean2[:, ds(g * GB, GB)], moments2[:, p, :, 0])
                pool.wait_ge(var2_ready, g + 1)
                pool.tensor_tensor(rstd2[:, ds(g * GB, GB)], var_eps2[:, p, :], minus_half[:],
                                   ALU.pow).then_inc(rstd2_ready, 1)

            def gate_wv(g, p):
                pool.wait_ge(gate_in[p], dma_count(g, p))
                reuse(pool, v_done, g - 1)
                pool.tensor_tensor(wv_gated[:, p, :].rearrange("k (b n) -> k b n", b=GB),
                                   wv[:].unsqueeze(1).to_broadcast([P, GB, P]),
                                   gate1[:, ds(g, 1), 0, :].rearrange("s a (b n) -> s (a b) n", b=GB),
                                   ALU.mult).then_inc(wv_gated_ready, 1)

            def residual_bias(g, p):
                reuse(pool, x1_ready, g - 1)
                pool.tensor_tensor(x_bias[:, p, :], x_all[:, ds(g * GW, GW)],
                                   gate1[:, ds(g, 1), 1, :].rearrange("s a n -> s (a n)"),
                                   ALU.add).then_inc(x_bias_ready, 1)

            def per_seq(stat, g):
                return stat[:, ds(g * GB, GB)].unsqueeze(2).to_broadcast([P, GB, P])

            def normalize2(g, p):
                pool.wait_ge(rstd2_ready, g + 1)
                pool.wait_ge(x1_ready, g + 1)
                reuse(pool, n2_ready, g)
                pool.tensor_tensor(x1_centred[:].rearrange("s (b n) -> s b n", b=GB),
                                   x1_all[:, ds(g * GW, GW)].rearrange("s (b n) -> s b n", b=GB),
                                   per_seq(mean2, g), ALU.subtract).then_inc(centred, 1)
                pool.wait_ge(centred, g + 1)
                reuse(pool, n2T_ready, g - 1)
                pool.tensor_tensor(n2_tok[:, p, :].rearrange("s (b n) -> s b n", b=GB),
                                   x1_centred[:].rearrange("s (b n) -> s b n", b=GB),
                                   per_seq(rstd2, g), ALU.mult).then_inc(n2_ready, 1)

            def split_act1(g):
                for j in range(0, HC, 2):
                    pool.wait_ge(act1_hi_ready, HC * g + j + 1)
                    pool.tensor_tensor(act1_lo[:, j, :], act1[:, j, :], act1_hi[:, j, :].bitcast(F32),
                                       ALU.subtract).then_inc(act1_lo_pool, 1)

            def phase_a(i, p):
                if isinstance(i, int) and i == G - 2:
                    normalize2(0, 0)
                if inside(i + 2):
                    rsqrt1(i + 2, p)
                    gate_wv(i + 2, p)
                if inside(i):
                    residual_bias(i, p)
                if isinstance(i, int) and i == G - 1:
                    normalize2(1, 1)
                if inside(i - 1):
                    rsqrt2(i - 1, 1 - p)

            def phase_b(i, p):
                if inside(i + 2):
                    normalize2(i + 2, p)
                if inside(i + 1):
                    split_act1(i + 1)

            rsqrt1(0, 0)
            pool.wait_ge(w1_hi_ready, 1)
            pool.tensor_tensor(w1_lo[:], w1[:], w1_hi[:].bitcast(F32), ALU.subtract).then_inc(w_split, 1)
            pool.wait_ge(w2_hi_ready, 1)
            pool.tensor_tensor(w2_lo[:], w2[:], w2_hi[:].bitcast(F32), ALU.subtract).then_inc(w_split, 1)
            pool.wait_ge(wv_in, 16)
            gate_wv(0, 0)
            steps(pool, phase_a, -1, G)
            split_act1(0)
            steps(pool, phase_b, 0, G - 2)

        @block.scalar
        def _(act):
            act.dma_start(tc_rows[:, 0, :], t).then_inc(tc_in, 16)
            act.dma_start(tc_rows[:, 1, :], c).then_inc(tc_in, 16)
            wc_dram = Wc.rearrange("(k p) m -> p k m", p=P)
            for first, last, arrived in ((A1, G1, wc_gate_in), (G1, A2, wc_mod1_in)):
                act.dma_start(wc[:, :, first * P:last * P], wc_dram[:, :, first * P:last * P])\
                    .then_inc(arrived, 16)
            act.dma_start(wq[:], Wq).then_inc(qk_in, 16)
            act.dma_start(wk[:], Wk).then_inc(qk_in, 16)
            act.dma_start(wc[:, :, A2 * P:MC * P], wc_dram[:, :, A2 * P:MC * P]).then_inc(wc_rest_in, 16)
            act.dma_start(w1[:], W1).then_inc(w1_in, 16)
            act.dma_start(w2[:], W2.rearrange("(k p) d -> p k d", p=P)).then_inc(w2_in, 16)

            def modulate(g, src, scale, shift, dest, done):
                for b in range(GB):
                    last = act.activation(dest[:, seq(b)], src[:, seq(b)], ACT.Identity,
                                          bias=shift[:, ds(g * GB + b, 1)], scale=scale[:, ds(g * GB + b, 1)])
                last.then_inc(done, 1)

            def modulate1(g, p):
                act.wait_ge(nT_ready, g + 1)
                reuse(act, v_done, g - 1)
                modulate(g, ps_nT, scale1, shift1, hT[:, p, :], hT_ready)

            def modulate2(g):
                act.wait_ge(n2T_ready, g + 1)
                modulate(g, ps_n2T, scale2, shift2, h2, h2_ready)

            def gelu1(g):
                for j in range(HC):
                    act.wait_ge(hid_done, HC * g + j + 1)
                    act.activation(act1[:, j, :], ps_hid[j][:], ACT.Gelu,
                                   bias=col_b(B1 + j)).then_inc(act1_ready, 1)

            def phase_a(i, p):
                q = 1 - p
                if inside(i):
                    act.wait_ge(max_ready, i + 1)
                    reuse(act, pT_done, i - 1)
                    reuse(act, inv_ready, i - 1)
                    for b in range(GB):
                        last = act.activation(probs[:, p, seq(b)], ps_s[:, seq(b)], ACT.Exp,
                                              bias=neg_max[:, p, b:b + 1],
                                              accum_out=row_sum[:, p, b:b + 1])
                    last.then_inc(probs_ready, 1)
                if inside(i + 1):
                    act.wait_ge(q_done, i + 2)
                    reuse(act, scores_done, i)
                    act.activation(qT[:, q, :], ps_q[:], ACT.Identity, bias=bq_scaled[:],
                                   scale=SCALE).then_inc(qT_ready, 1)
                    act.wait_ge(k_done, i + 2)
                    act.activation(kT[:, q, :], ps_k[:], ACT.Identity, bias=col_a(BK)).then_inc(kT_ready, 1)
                    act.wait_ge(v_done, i + 2)
                    reuse(act, o_done, i)
                    act.activation(v_tok[:, q, :], ps_v[:], ACT.Copy).then_inc(v_ready, 1)
                if inside(i):
                    act.wait_ge(pT_done, i + 1)
                    act.activation(pT[:, p, :], ps_pT[:], ACT.Copy).then_inc(pT_ready, 1)
                if inside(i + 2):
                    modulate1(i + 2, p)
                if isinstance(i, int) and i == G - 1:
                    act.wait_ge(mod2_ready, 3)
                    modulate2(0)

            def phase_b(i, p):
                if inside(i):
                    act.wait_ge(y_done, i + 1)
                    act.activation(act2[:, p, :], ps_y[:], ACT.Gelu, bias=col_b(B2)).then_inc(act2_ready, 1)
                if inside(i + 1):
                    gelu1(i + 1)
                if inside(i + 2):
                    modulate2(i + 2)
                if inside(i):
                    act.wait_ge(act2_ready, i + 1)
                    reuse(act, oT_done, i)
                    for b in range(GB):
                        last = act.activation(act2_gated[:, seq(b)], act2[:, p, seq(b)], ACT.Copy,
                                              scale=a2[:, ds(i * GB + b, 1)])
                    last.then_inc(gated_ready, 1)

            act.preload_act_table(ACT.Exp)
            act.wait_ge(w1_in, 16)
            act.activation(w1_hi[:], w1[:], ACT.Copy).then_inc(w1_hi_ready, 1)
            act.wait_ge(w2_in, 16)
            act.activation(w2_hi[:], w2[:], ACT.Copy).then_inc(w2_hi_ready, 1)
            act.wait_ge(mod1_ready, 2)
            modulate1(0, 0)
            act.wait_ge(bq_ready, 1)
            steps(act, phase_a, -1, G - 1)
            gelu1(0)
            modulate2(1)
            steps(act, phase_b, 0, G - 1)

        @block.vector
        def _(dve):
            def stats1(g, p, between=None):
                dve.wait_ge(x_in[p], dma_count(g, p))
                for b in range(GB):
                    last = dve.bn_stats(stats[:, p, b, :], x_all[:, ds(g * GW + b * P, P)])
                last.then_inc(stats_done, 1)
                dve.wait_ge(stats_done, g + 1)
                if between:
                    between()
                for b in range(GB):
                    last = dve.bn_aggr(moments[:, p, b, :], stats[:, p, b, :])
                last.then_inc(moments_ready, 1)

            def normalize1(g, p, sequences):
                dve.wait_ge(rstd_ready, g + 1)
                reuse(dve, nT_ready, g - 1)
                for b in sequences:
                    last = dve.tensor_scalar(n_tok[:, p, seq(b)], x_all[:, ds(g * GW + b * P, P)],
                                             moments[:, p, b, 0:1], rstd[:, p, b:b + 1],
                                             ALU.subtract, ALU.mult)
                return last

            def split_h2(g):
                dve.wait_ge(h2_ready, g + 1)
                dve.tensor_copy(h2_hi[:], h2[:]).then_inc(h2_hi_ready, 1)
                dve.wait_ge(h2_hi_ready, g + 1)
                dve.tensor_tensor(h2_lo[:], h2[:], h2_hi[:].bitcast(F32), ALU.subtract).then_inc(h2_split, 1)

            def split_act1(g):
                for j in range(HC):
                    dve.wait_ge(act1_ready, HC * g + j + 1)
                    dve.tensor_copy(act1_hi[:, j, :], act1[:, j, :]).then_inc(act1_hi_ready, 1)
                    if j % 2:
                        dve.wait_ge(act1_hi_ready, HC * g + j + 1)
                        dve.tensor_tensor(act1_lo[:, j, :], act1[:, j, :], act1_hi[:, j, :].bitcast(F32),
                                          ALU.subtract).then_inc(act1_lo_dve, 1)

            def phase_a(i, p):
                q = 1 - p
                def invert_sums():
                    if inside(i - 1):
                        dve.wait_ge(probs_ready, i)
                        dve.reciprocal(inv_sum[:, q, :], row_sum[:, q, :]).then_inc(inv_ready, 1)

                if inside(i + 2):
                    stats1(i + 2, p, invert_sums)
                else:
                    invert_sums()
                if inside(i):
                    dve.wait_ge(scores_done, i + 1)
                    reuse(dve, probs_ready, i - 1)
                    dve.tensor_reduce(neg_max[:, p, :], ps_s[:].rearrange("s (b t) -> s b t", b=GB),
                                      AX_X, ALU.max, negate=True).then_inc(max_ready, 1)
                if inside(i - 1):
                    dve.wait_ge(inv_ready, i)
                    dve.wait_ge(x_bias_ready, i)
                    dve.wait_ge(o_done, i)
                    for b in range(GB):
                        last = dve.scalar_tensor_tensor(x1_all[:, ds((i - 1) * GW + b * P, P)],
                                                        ps_o[:, seq(b)], inv_sum[:, q, b:b + 1],
                                                        x_bias[:, q, seq(b)], ALU.mult, ALU.add)
                    last.then_inc(x1_ready, 1)
                    dve.wait_ge(x1_ready, i)
                if inside(i + 2):
                    normalize1(i + 2, p, range(0, GB // 2))
                if inside(i - 1):
                    for b in range(GB):
                        last = dve.bn_stats(stats2[:, q, b, :], x1_all[:, ds((i - 1) * GW + b * P, P)])
                    last.then_inc(stats2_done, 1)
                    dve.wait_ge(stats2_done, i)
                if inside(i + 2):
                    normalize1(i + 2, p, range(GB // 2, GB)).then_inc(n_ready, 1)
                if inside(i - 1):
                    for b in range(GB):
                        last = dve.bn_aggr(moments2[:, q, b, :], stats2[:, q, b, :])
                    last.then_inc(moments2_ready, 1)

            def phase_b(i, p):
                q = 1 - p
                if inside(i - 1):
                    dve.wait_ge(oT_done, i)
                    dve.wait_ge(stored[q], dma_count(i - 1, q))
                    dve.tensor_tensor(out_tok[:, q, :], ps_oT[:], x1_all[:, ds((i - 1) * GW, GW)],
                                      ALU.add).then_inc(out_ready, 1)
                if inside(i + 1):
                    split_act1(i + 1)
                if inside(i + 2):
                    split_h2(i + 2)

            def gain(n, m):
                return dve.tensor_scalar(one_g[:, n, :], cond(m), col_a(BC + m), 1.0, ALU.add, ALU.add)

            dve.wait_ge(tc_done, 1)
            dve.tensor_copy(tc_T[:].rearrange("p k b -> p (k b)"), ps_tc[:, 0:KC * B]).then_inc(tc_ready, 1)
            dve.wait_ge(gate_done, 1)
            dve.wait_ge(bc_row_in, 16)
            dve.tensor_tensor(gate_rows[:, 0, :], ps_gate[0:B, 0:P], bc_row[:], ALU.add).then_inc(gate_row, 1)
            dve.wait_ge(bv_row_in, 16)
            dve.wait_ge(gate_row, 1)
            dve.tensor_tensor(gate_rows[:, 1, :], gate_rows[:, 0, :], bv_row[:], ALU.mult)\
                .then_inc(gate_rows_ready, 1)
            stats1(0, 0)
            normalize1(0, 0, range(GB)).then_inc(n_ready, 1)
            dve.wait_ge(cols_a_T, 1)
            dve.tensor_copy(cols_a[:], ps_vec[:, 0:NA]).then_inc(cols_a_ready, 1)
            dve.wait_ge(cols_a_ready, 1)
            dve.tensor_scalar(bq_scaled[:], col_a(BQ), SCALE, None, ALU.mult).then_inc(bq_ready, 1)
            dve.wait_ge(cond1_done, 1)
            gain(0, G1).then_inc(mod1_step, 1)
            dve.wait_ge(mod1_step, 1)
            dve.tensor_scalar(scale1[:], one_g[:, 0, :], col_a(LG1), None, ALU.mult).then_inc(mod1_ready, 1)
            dve.tensor_scalar(shift_part[:, 0, :], one_g[:, 0, :], col_a(LB1), col_a(BC + BE1), ALU.mult,
                              ALU.add).then_inc(mod1_step, 1)
            dve.wait_ge(mod1_step, 2)
            dve.tensor_tensor(shift1[:], cond(BE1), shift_part[:, 0, :], ALU.add).then_inc(mod1_ready, 1)
            phase_a(-1, 1)
            dve.wait_ge(cond2_done, 1)
            dve.tensor_copy(cols_b[:], ps_late[:, cols_b_at:cols_b_at + NB]).then_inc(cols_b_ready, 1)
            gain(1, G2).then_inc(mod2_step, 1)
            dve.wait_ge(cols_b_ready, 1)
            dve.wait_ge(mod2_step, 1)
            dve.tensor_scalar(scale2[:], one_g[:, 1, :], col_b(LG2), None, ALU.mult).then_inc(mod2_ready, 1)
            dve.tensor_scalar(shift_part[:, 1, :], one_g[:, 1, :], col_b(LB2), None, ALU.mult).then_inc(mod2_step, 1)
            dve.wait_ge(mod2_step, 2)
            dve.scalar_tensor_tensor(shift2[:], cond(BE2), col_a(BC + BE2), shift_part[:, 1, :], ALU.add,
                                     ALU.add).then_inc(mod2_ready, 1)
            dve.tensor_scalar(a2[:], cond(A2), col_a(BC + A2), None, ALU.add).then_inc(mod2_ready, 1)

            steps(dve, phase_a, 0, G - 1)
            split_h2(0)
            phase_a(G, G % 2)
            split_act1(0)
            split_h2(1)
            steps(dve, phase_b, 0, G)

        @block.tensor
        def _(pe):
            def transpose_group(dest, src, done):
                for b in range(GB):
                    last = pe.transpose(dest[:, seq(b)], src[:, seq(b)], ident[:])
                last.then_inc(done, 1)

            def split_product(dest, w_hi, w_lo, m_hi, m_lo, start, stop):
                pe.matmul(dest, w_lo, m_hi, start=start, stop=False)
                pe.matmul(dest, w_hi, m_hi, start=False, stop=False)
                return pe.matmul(dest, w_hi, m_lo, start=False, stop=stop)

            def transpose_n1(g, p):
                pe.wait_ge(n_ready, g + 1)
                reuse(pe, hT_ready, g)
                transpose_group(ps_nT, n_tok[:, p, :], nT_ready)

            def transpose_n2(g, p):
                pe.wait_ge(n2_ready, g + 1)
                transpose_group(ps_n2T, n2_tok[:, p, :], n2T_ready)

            def up(g):
                pe.wait_ge(h2_split, g + 1)
                for j in range(HC):
                    split_product(ps_hid[j][:], w1_hi[:, seq(j)], w1_lo[:, seq(j)], h2_hi[:],
                                  h2_lo[:], start=True, stop=True).then_inc(hid_done, 1)

            def down(g):
                reuse(pe, act2_ready, g)
                for j in range(HC):
                    if j % 2:
                        pe.wait_ge(act1_lo_dve, HC // 2 * g + j // 2 + 1)
                    else:
                        pe.wait_ge(act1_lo_pool, HC // 2 * g + j // 2 + 1)
                    last = split_product(ps_y[:], w2_hi[:, j, :], w2_lo[:, j, :], act1_hi[:, j, :],
                                         act1_lo[:, j, :], start=j == 0, stop=j == HC - 1)
                last.then_inc(y_done, 1)

            def phase_a(i, p):
                q = 1 - p
                if inside(i):
                    pe.wait_ge(qT_ready, i + 1)
                    pe.wait_ge(kT_ready, i + 1)
                    reuse(pe, probs_ready, i)
                    for b in range(GB):
                        last = pe.matmul(ps_s[:, seq(b)], qT[:, p, seq(b)], kT[:, p, seq(b)],
                                         start=True, stop=True)
                    last.then_inc(scores_done, 1)
                if inside(i - 1):
                    pe.wait_ge(pT_ready, i)
                    pe.wait_ge(v_ready, i)
                    reuse(pe, x1_ready, i - 1)
                    for b in range(GB):
                        last = pe.matmul(ps_o[:, seq(b)], pT[:, q, seq(b)], v_tok[:, q, seq(b)],
                                         start=True, stop=True)
                    last.then_inc(o_done, 1)
                if inside(i + 1):
                    pe.wait_ge(hT_ready, i + 2)
                    reuse(pe, qT_ready, i + 1)
                    pe.matmul(ps_q[:], wq[:], hT[:, q, :], start=True, stop=True).then_inc(q_done, 1)
                    reuse(pe, kT_ready, i + 1)
                    pe.matmul(ps_k[:], wk[:], hT[:, q, :], start=True, stop=True).then_inc(k_done, 1)
                    pe.wait_ge(wv_gated_ready, i + 2)
                    reuse(pe, v_ready, i + 1)
                    for b in range(GB):
                        last = pe.matmul(ps_v[:, seq(b)], hT[:, q, seq(b)], wv_gated[:, q, seq(b)],
                                         start=True, stop=True)
                    last.then_inc(v_done, 1)
                if isinstance(i, int) and i == G - 1:
                    transpose_n2(0, 0)
                if inside(i):
                    pe.wait_ge(probs_ready, i + 1)
                    reuse(pe, pT_ready, i)
                    transpose_group(ps_pT, probs[:, p, :], pT_done)
                if inside(i + 2):
                    transpose_n1(i + 2, p)

            def phase_b(i, p):
                if inside(i):
                    down(i)
                if inside(i - 1):
                    pe.wait_ge(gated_ready, i)
                    reuse(pe, out_ready, i - 1)
                    transpose_group(ps_oT, act2_gated, oT_done)
                if inside(i + 1):
                    up(i + 1)
                if inside(i + 2):
                    transpose_n2(i + 2, p)

            def project_cond(m):
                for k in range(KC):
                    last = pe.matmul(cond(m), wc[:, k, seq(m)], tc_T[:, k, :],
                                     start=k == 0, stop=k == KC - 1)
                return last

            pe.wait_ge(consts_ready, 1)
            pe.wait_ge(tc_in, 32)
            for k in range(KC):
                last = pe.transpose(ps_tc[:, k * B:(k + 1) * B], tc_rows[:, k, :], ident[0:B, 0:B])
            last.then_inc(tc_done, 1)
            pe.wait_ge(tc_ready, 1)
            pe.wait_ge(wc_gate_in, 16)
            for k in range(KC):
                last = pe.matmul(ps_gate[0:B, 0:P], tc_T[:, k, :], wc[:, k, seq(A1)],
                                 start=k == 0, stop=k == KC - 1)
            last.then_inc(gate_done, 1)
            pe.wait_ge(wc_mod1_in, 16)
            project_cond(G1)
            project_cond(BE1).then_inc(cond1_done, 1)
            transpose_n1(0, 0)
            pe.wait_ge(cols_a_in, 16 * 5)
            pe.transpose(ps_vec[:, 0:NA], rows_a[:], ident[0:NA, 0:NA]).then_inc(cols_a_T, 1)
            pe.wait_ge(cols_b_in, 16 * 4)
            pe.transpose(ps_late[:, cols_b_at:cols_b_at + NB], rows_b[:], ident[0:NB, 0:NB])
            pe.wait_ge(wc_rest_in, 16)
            for m in (A2, G2, BE2):
                last = project_cond(m)
            last.then_inc(cond2_done, 1)
            pe.wait_ge(qk_in, 32)
            steps(pe, phase_a, -1, G)
            pe.wait_ge(w_split, 2)
            up(0)
            transpose_n2(1, 1)
            steps(pe, phase_b, 0, G)


_INS = ["x", "fside_BxS_0", "cond_1024"] + [
    "L0_cond_" + n for n in ("Wq", "bq", "Wk", "bk", "Wv", "bv", "W1", "b1", "W2", "b2", "Wc", "bc",
                             "ln1_g", "ln1_b", "ln2_g", "ln2_b")]


def kernel(**inputs):
    import numpy as _np
    import concourse.bacc as _bacc
    from concourse import mybir as _mybir
    from concourse.bass_utils import run_bass_kernel_spmd as _run

    nc = _bacc.Bacc("TRN2", target_bir_lowering=False, num_devices=1)
    arrays, args = {}, []
    for name in _INS:
        a = _np.ascontiguousarray(inputs[name])
        arrays[f"in_{name}"] = a
        args.append(nc.dram_tensor(f"in_{name}", a.shape, _mybir.dt.from_np(a.dtype), kind="ExternalInput").ap())
    out = nc.dram_tensor("out_x", arrays["in_x"].shape, _mybir.dt.float32, kind="ExternalOutput").ap()
    cond_block_kernel(nc, *args, out)
    r = _run(nc, [arrays], core_ids=[0])
    return r.results[0]["out_x"]
```

```python
from contextlib import ExitStack

import concourse.bass as bass
from concourse import mybir

F32 = mybir.dt.float32
F32R = mybir.dt.float32r
ALU = mybir.AluOpType
ACT = mybir.ActivationFunctionType
AX_X = mybir.AxisListType.X
ds = bass.ds

P = 128
GB = 4
GW = GB * P
EPS = 1e-5
WARM = (6, 2, 1, 2, 5)
LOOP_FROM = 2
LOOP_PAIRS = 2


def cond_block_kernel(nc, x, t, c, Wq, bq, Wk, bk, Wv, bv, W1, b1, W2, b2, Wc, bc,
                      ln1_g, ln1_b, ln2_g, ln2_b, out):
    B, S, D = x.shape
    assert S == P and D == P and B % GB == 0
    G = B // GB
    HC = W1.shape[1] // P
    KC = Wc.shape[0] // P
    MC = Wc.shape[1] // P
    SCALE = float(D) ** -0.5
    A1, G1, BE1, A2, G2, BE2 = range(MC)
    BC, LG1, LB1, BQ, BK = 0, *range(MC, MC + 4)
    NA = BK + 1
    B2, LG2, LB2, B1 = range(4)
    NB = B1 + HC

    POOL_CHUNKS = (1,)
    DVE_CHUNKS = tuple(j for j in range(HC) if j not in POOL_CHUNKS)

    def inside(g):
        return 0 <= g < G if isinstance(g, int) else True

    def steps(eng, step, first, last):
        after = LOOP_FROM + 2 * LOOP_PAIRS
        for i in range(first, LOOP_FROM):
            step(i, i % 2)
        with eng.Fori(0, LOOP_PAIRS) as r:
            for u in range(2):
                step(2 * r + (LOOP_FROM + u), (LOOP_FROM + u) % 2)
        for i in range(after, last + 1):
            step(i, i % 2)

    def reuse(eng, semaphore, value):
        if not isinstance(value, int) or value > 0:
            eng.wait_ge(semaphore, value)

    with ExitStack() as ctx:
        def sb(name, shape, dt=F32):
            return ctx.enter_context(nc.sbuf_tensor(name, shape, dt))

        def sem(name):
            return ctx.enter_context(nc.semaphore(name))

        x_all = sb("x_all", [P, G * GW])
        x1_all = sb("x1_all", [P, G * GW])
        gate1 = sb("gate1", [P, G, 2, GW])
        ident = sb("ident", [P, P])
        wq, wk, wv = (sb(n, [P, P]) for n in ("wq", "wk", "wv"))
        w1 = sb("w1", [P, HC * P])
        w2 = sb("w2", [P, HC, P])
        w1_hi, w1_lo = (sb(n, [P, HC * P], F32R) for n in ("w1_hi", "w1_lo"))
        w2_hi, w2_lo = (sb(n, [P, HC, P], F32R) for n in ("w2_hi", "w2_lo"))
        wc = sb("wc", [P, KC, MC * P])
        rows_a, rows_b = sb("rows_a", [NA, P]), sb("rows_b", [NB, P])
        cols_a, cols_b = sb("cols_a", [P, NA]), sb("cols_b", [P, NB])
        bq_scaled = sb("bq_scaled", [P, 1])
        tc_rows = sb("tc_rows", [B, KC, P])
        tc_T = sb("tc_T", [P, KC, B])
        bv_row = sb("bv_row", [B, P])
        ones_row = sb("ones_row", [1, B])
        gate_rows = sb("gate_rows", [B, 2, P])
        one_g = sb("one_g", [P, 2, B])
        shift_part = sb("shift_part", [P, 2, B])
        scale1, shift1, scale2, shift2, a2 = (
            sb(n, [P, B]) for n in ("scale1", "shift1", "scale2", "shift2", "a2"))
        mean2, rstd2 = sb("mean2", [P, B]), sb("rstd2", [P, B])
        eps = sb("eps", [P, GB])
        minus_half = sb("minus_half", [P, GB])
        stats, stats2 = (sb(n, [P, 2, GB, 6]) for n in ("stats", "stats2"))
        moments, moments2 = (sb(n, [P, 2, GB, 2]) for n in ("moments", "moments2"))
        var_eps, var_eps2 = (sb(n, [P, 2, GB]) for n in ("var_eps", "var_eps2"))
        wv_gated = sb("wv_gated", [P, 2, GW])
        n2_tok = sb("n2_tok", [P, 2, GW])
        rstd = sb("rstd", [P, 2, GB])
        n_tok = sb("n_tok", [P, 2, GW])
        hT = sb("hT", [P, 2, GW])
        qT = sb("qT", [P, 2, GW])
        kT = sb("kT", [P, 2, GW])
        v_tok = sb("v_tok", [P, 2, GW])
        neg_max = sb("neg_max", [P, 2, GB])
        probs = sb("probs", [P, 2, GW])
        row_sum = sb("row_sum", [P, 2, GB])
        inv_sum = sb("inv_sum", [P, 2, GB])
        pT = sb("pT", [P, 2, GW])
        x_bias = sb("x_bias", [P, 2, GW])
        act2 = sb("act2", [P, 2, GW])
        out_tok = sb("out_tok", [P, 2, GW])
        x1_centred = sb("x1_centred", [P, GW])
        h2 = sb("h2", [P, GW])
        h2_hi, h2_lo = (sb(n, [P, GW], F32R) for n in ("h2_hi", "h2_lo"))
        act1 = sb("act1", [P, HC, GW])
        act1_hi, act1_lo = (sb(n, [P, HC, GW], F32R) for n in ("act1_hi", "act1_lo"))
        act2_gated = sb("act2_gated", [P, GW])
        out_last = sb("out_last", [P, GW])
        gate_dram = nc.dram_tensor("gate_dram", [2, B, P], F32, kind="Internal").ap()

        bank = [ctx.enter_context(nc.psum_tensor(f"bank{i}", [P, GW], F32)) for i in range(8)]
        ps_nT, ps_q, ps_k, ps_v, ps_s, ps_pT, ps_o, ps_vec = bank
        ps_n2T = ps_nT
        ps_hid = [bank[1], bank[2], bank[3], bank[7]]
        ps_y, ps_oT = ps_s, ps_pT
        ps_y_half, ps_oT_half = (ps_y, ps_hid[0]), (ps_hid[1], ps_hid[2])
        ps_tc, ps_late, ps_cond1, ps_gate = ps_o, ps_o, ps_pT, ps_s

        x_in = [sem("x_in0"), sem("x_in1")]
        gate_in = [sem("gate_in0"), sem("gate_in1")]
        cols_a_in, bqk_in, ln2_in, cols_b_in, tc_in, qk_in, wv_in, bc_in, bv_row_in, w1_in, w2_in = (
            sem(n) for n in ("cols_a_in", "bqk_in", "ln2_in", "cols_b_in", "tc_in", "qk_in", "wv_in", "bc_in",
                             "bv_row_in", "w1_in", "w2_in"))
        wc_gate_in, wc_mod1_in, wc_rest_in = (
            sem(n) for n in ("wc_gate_in", "wc_mod1_in", "wc_rest_in"))
        zeroed, consts_ready = sem("zeroed"), sem("consts_ready")
        cols_a_T, cols_b_T, tc_done, cond1_done, cond2_done, gate_done = (
            sem(n) for n in ("cols_a_T", "cols_b_T", "tc_done", "cond1_done", "cond2_done",
                             "gate_done"))
        cols_a_ready, cols_b_ready, tc_ready, bq_ready, mod1_step, mod1_ready, mod2_step, mod2_ready = (
            sem(n) for n in ("cols_a_ready", "cols_b_ready", "tc_ready", "bq_ready", "mod1_step",
                             "mod1_ready", "mod2_step", "mod2_ready"))
        gate_rows_ready, gate_stored = (
            sem(n) for n in ("gate_rows_ready", "gate_stored"))
        w1_hi_ready, w2_hi_ready, w_split = sem("w1_hi_ready"), sem("w2_hi_ready"), sem("w_split")
        stats_done, moments_ready, var_ready, rstd_ready, n_ready, nT_ready = (
            sem(n) for n in ("stats_done", "moments_ready", "var_ready", "rstd_ready", "n_ready",
                             "nT_ready"))
        stats2_done, moments2_ready, var2_ready, rstd2_ready, centred, n2_ready, n2T_ready = (
            sem(n) for n in ("stats2_done", "moments2_ready", "var2_ready", "rstd2_ready", "centred",
                             "n2_ready", "n2T_ready"))
        wv_gated_ready = sem("wv_gated_ready")
        hT_ready, q_done, k_done, v_done, qT_ready, kT_ready, v_ready = (
            sem(n) for n in ("hT_ready", "q_done", "k_done", "v_done", "qT_ready", "kT_ready",
                             "v_ready"))
        scores_done, max_ready, probs_ready, pT_done, pT_ready, o_done = (
            sem(n) for n in ("scores_done", "max_ready", "probs_ready", "pT_done", "pT_ready",
                             "o_done"))
        x_bias_ready, inv_ready, x1_ready = (
            sem(n) for n in ("x_bias_ready", "inv_ready", "x1_ready"))
        h2_ready, h2_hi_ready, h2_split = (
            sem(n) for n in ("h2_ready", "h2_hi_ready", "h2_split"))
        hid_done, act1_ready, act1_hi_ready = (
            sem(n) for n in ("hid_done", "act1_ready", "act1_hi_ready"))
        act1_lo_pool, act1_lo_dve = sem("act1_lo_pool"), sem("act1_lo_dve")
        y_done, act2_ready, gated_ready, oT_done, out_ready = (
            sem(n) for n in ("y_done", "act2_ready", "gated_ready", "oT_done", "out_ready"))
        gated_half = sem("gated_half")
        stored = [sem("stored0"), sem("stored1")]

        def col_a(i):
            return cols_a[:, i:i + 1]

        def col_b(i):
            return cols_b[:, i:i + 1]

        def seq(b):
            return slice(b * P, (b + 1) * P)

        def half_of(h):
            return slice(h * GW // 2, (h + 1) * GW // 2)

        def dma_count(g, p):
            return 8 * (g - p) + 16

        def cond(m):
            return (ps_cond1 if m in (G1, BE1) else ps_late)[:, m * B:(m + 1) * B]

        cols_b_at = MC * B

        block = ctx.enter_context(nc.Block())

        @block.sync
        def _(sp):
            def load_x(g, p):
                sp.dma_start(x_all[:, ds(g * GW, GW)].rearrange("s (b d) -> s b d", b=GB),
                             x[ds(g * GB, GB)].rearrange("b s d -> s b d")).then_inc(x_in[p], 16)

            def load_gate(g, p):
                sp.dma_start(gate1[:, ds(g, 1), :, :].rearrange("s a k n -> s (a k) n"),
                             gate_dram[:, ds(g * GB, GB), :].rearrange("k b d -> k (b d)")
                             .partition_broadcast(P)).then_inc(gate_in[p], 16)

            def row(v):
                return v.rearrange("(a d) -> a d", d=P)

            for u in range(2):
                sp.sem_inc(stored[u], 16)
            load_x(0, 0)
            sp.dma_start(rows_a[BC:BC + MC, :], row(bc)).then_inc(bc_in, 16)
            for i, v in ((LG1, ln1_g), (LB1, ln1_b)):
                sp.dma_start(rows_a[i:i + 1, :], row(v)).then_inc(cols_a_in, 16)
            load_x(1, 1)
            sp.dma_start(wv[:], Wv).then_inc(wv_in, 16)
            sp.wait_ge(gate_rows_ready, 1)
            sp.dma_start(gate_dram.rearrange("k b d -> b k d"), gate_rows[:]).then_inc(gate_stored, 16)
            sp.wait_ge(x_in[0], 16)
            load_x(2, 0)
            sp.dma_start(rows_b[B1:B1 + HC, :], row(b1)).then_inc(cols_b_in, 16)
            sp.dma_start(rows_b[B2:B2 + 1, :], row(b2)).then_inc(cols_b_in, 16)
            sp.wait_ge(gate_stored, 16)
            load_gate(0, 0)
            load_gate(1, 1)
            sp.dma_start(w1[:], W1).then_inc(w1_in, 16)
            sp.wait_ge(x_in[1], 16)
            load_x(3, 1)
            with sp.Fori(0, G // 2 - 2) as r:
                for u in range(2):
                    g = 2 * r + (2 + u)
                    sp.wait_ge(gate_in[u], dma_count(g - 2, u))
                    load_gate(g, u)
                    sp.wait_ge(x_in[u], dma_count(g, u))
                    load_x(g + 2, u)
            for u in range(2):
                sp.wait_ge(gate_in[u], dma_count(G - 4 + u, u))
                load_gate(G - 2 + u, u)
            def store(first, count, src, u):
                sp.dma_start(out[ds(first, count)].rearrange("b s d -> s b d"),
                             src.rearrange("s (b d) -> s b d", b=count)).then_inc(stored[u], 16)

            with sp.Fori(0, G // 2 - 1) as r:
                for u in range(2):
                    sp.wait_ge(out_ready, 2 * r + (u + 1))
                    store((2 * r + u) * GB, GB, out_tok[:, u, :], u)
            sp.wait_ge(out_ready, G - 1)
            store((G - 2) * GB, GB, out_tok[:, 0, :], 0)
            for h in range(2):
                sp.wait_ge(out_ready, G + h)
                store((G - 1) * GB + h * GB // 2, GB // 2, out_last[:, half_of(h)], 1)
            sp.wait_ge(stored[0], 16 * (G // 2 + 1))
            sp.wait_ge(stored[1], 16 * (G // 2 + 2))

        @block.gpsimd
        def _(pool):
            pool.memset(ident[:], 0.0).then_inc(zeroed, 1)
            pool.memset(ones_row[:], 1.0)
            pool.memset(eps[:], EPS)
            pool.memset(minus_half[:], -0.5)
            pool.wait_ge(zeroed, 1)
            pool.affine_select(out=ident[:], in_=ident[:], compare_op=ALU.not_equal, fill=1.0, base=0,
                               pattern=[[-1, P]], channel_multiplier=1).then_inc(consts_ready, 1)
            pool.dma_start(bv_row[:], bv.partition_broadcast(B)).then_inc(bv_row_in, 16)
            for i, v in ((BQ, bq), (BK, bk)):
                pool.dma_start(rows_a[i:i + 1, :], v.rearrange("(a d) -> a d", a=1)).then_inc(bqk_in, 16)

            def rsqrt1(g, p):
                pool.wait_ge(moments_ready, g + 1)
                pool.tensor_tensor(var_eps[:, p, :], moments[:, p, :, 1], eps[:], ALU.add).then_inc(var_ready, 1)
                pool.wait_ge(var_ready, g + 1)
                pool.tensor_tensor(rstd[:, p, :], var_eps[:, p, :], minus_half[:], ALU.pow).then_inc(rstd_ready, 1)

            def rsqrt2(g, p):
                pool.wait_ge(moments2_ready, g + 1)
                pool.tensor_tensor(var_eps2[:, p, :], moments2[:, p, :, 1], eps[:], ALU.add).then_inc(var2_ready, 1)
                pool.tensor_copy(mean2[:, ds(g * GB, GB)], moments2[:, p, :, 0])
                pool.wait_ge(var2_ready, g + 1)
                pool.tensor_tensor(rstd2[:, ds(g * GB, GB)], var_eps2[:, p, :], minus_half[:],
                                   ALU.pow).then_inc(rstd2_ready, 1)

            def gate_wv(g, p):
                pool.wait_ge(gate_in[p], dma_count(g, p))
                reuse(pool, v_done, g - 1)
                pool.tensor_tensor(wv_gated[:, p, :].rearrange("k (b n) -> k b n", b=GB),
                                   wv[:].unsqueeze(1).to_broadcast([P, GB, P]),
                                   gate1[:, ds(g, 1), 0, :].rearrange("s a (b n) -> s (a b) n", b=GB),
                                   ALU.mult).then_inc(wv_gated_ready, 1)

            def residual_bias(g, p):
                reuse(pool, x1_ready, g - 1)
                pool.tensor_tensor(x_bias[:, p, :], x_all[:, ds(g * GW, GW)],
                                   gate1[:, ds(g, 1), 1, :].rearrange("s a n -> s (a n)"),
                                   ALU.add).then_inc(x_bias_ready, 1)

            def per_seq(stat, g):
                return stat[:, ds(g * GB, GB)].unsqueeze(2).to_broadcast([P, GB, P])

            def normalize2(g, p):
                pool.wait_ge(rstd2_ready, g + 1)
                pool.wait_ge(x1_ready, g + 1)
                reuse(pool, n2_ready, g)
                pool.tensor_tensor(x1_centred[:].rearrange("s (b n) -> s b n", b=GB),
                                   x1_all[:, ds(g * GW, GW)].rearrange("s (b n) -> s b n", b=GB),
                                   per_seq(mean2, g), ALU.subtract).then_inc(centred, 1)
                pool.wait_ge(centred, g + 1)
                reuse(pool, n2T_ready, g - 1)
                pool.tensor_tensor(n2_tok[:, p, :].rearrange("s (b n) -> s b n", b=GB),
                                   x1_centred[:].rearrange("s (b n) -> s b n", b=GB),
                                   per_seq(rstd2, g), ALU.mult).then_inc(n2_ready, 1)

            def split_act1(g):
                for j in POOL_CHUNKS:
                    pool.wait_ge(act1_hi_ready, HC * g + j + 1)
                    pool.tensor_tensor(act1_lo[:, j, :], act1[:, j, :], act1_hi[:, j, :].bitcast(F32),
                                       ALU.subtract).then_inc(act1_lo_pool, 1)

            def phase_a(i, p):
                if isinstance(i, int) and i in (G - 2, G - 1):
                    normalize2(i - (G - 2), p)
                if inside(i + 2):
                    rsqrt1(i + 2, p)
                    gate_wv(i + 2, p)
                if inside(i):
                    residual_bias(i, p)
                if isinstance(i, int) and i == 0:
                    pool.wait_ge(w1_hi_ready, 1)
                    pool.tensor_tensor(w1_lo[:], w1[:], w1_hi[:].bitcast(F32), ALU.subtract).then_inc(w_split, 1)
                if isinstance(i, int) and i == 1:
                    pool.wait_ge(w2_hi_ready, 1)
                    pool.tensor_tensor(w2_lo[:], w2[:], w2_hi[:].bitcast(F32), ALU.subtract).then_inc(w_split, 1)
                if inside(i - 2):
                    rsqrt2(i - 2, p)

            def phase_b(i, p):
                if inside(i + 2):
                    normalize2(i + 2, p)
                if inside(i + 1):
                    split_act1(i + 1)
                if isinstance(i, int) and i < 2:
                    rsqrt2(G - 2 + i, i)

            rsqrt1(0, 0)
            for i, v in ((LG2, ln2_g), (LB2, ln2_b)):
                pool.dma_start(rows_b[i:i + 1, :], v.rearrange("(a d) -> a d", a=1)).then_inc(ln2_in, 16)
            rsqrt1(1, 1)
            pool.wait_ge(wv_in, 16)
            gate_wv(0, 0)
            gate_wv(1, 1)
            steps(pool, phase_a, 0, G - 1)
            split_act1(0)
            steps(pool, phase_b, 0, G - 2)

        @block.scalar
        def _(act):
            act.dma_start(tc_rows[:, 0, :], t).then_inc(tc_in, 16)
            act.dma_start(tc_rows[:, 1, :], c).then_inc(tc_in, 16)
            wc_dram = Wc.rearrange("(k p) m -> p k m", p=P)
            for first, last, arrived in ((A1, G1, wc_gate_in), (G1, A2, wc_mod1_in)):
                act.dma_start(wc[:, :, first * P:last * P], wc_dram[:, :, first * P:last * P])\
                    .then_inc(arrived, 16)
            act.dma_start(wq[:], Wq).then_inc(qk_in, 16)
            act.dma_start(wk[:], Wk).then_inc(qk_in, 16)

            def modulate(g, b, src, scale, shift, dest):
                return act.activation(dest[:, seq(b)], src[:, seq(b)], ACT.Identity,
                                      bias=shift[:, ds(g * GB + b, 1)], scale=scale[:, ds(g * GB + b, 1)])

            def modulate1(g, p):
                act.wait_ge(nT_ready, g + 1)
                reuse(act, v_done, g - 1)
                for half in range(2):
                    modulate(g, 2 * half, ps_nT, scale1, shift1, hT[:, p, :])
                    modulate(g, 2 * half + 1, ps_nT, scale1, shift1, hT[:, p, :]).then_inc(hT_ready, 1)

            def modulate2(g):
                act.wait_ge(n2T_ready, g + 1)
                reuse(act, h2_split, g)
                for b in range(GB):
                    last = modulate(g, b, ps_n2T, scale2, shift2, h2)
                last.then_inc(h2_ready, 1)

            def gelu1(g):
                for j in range(HC):
                    act.wait_ge(hid_done, HC * g + j + 1)
                    act.activation(act1[:, j, :], ps_hid[j][:], ACT.Gelu,
                                   bias=col_b(B1 + j)).then_inc(act1_ready, 1)

            def softmax(g, p):
                act.wait_ge(max_ready, g + 1)
                reuse(act, pT_done, g - 1)
                reuse(act, inv_ready, g - 1)
                for b in range(GB):
                    last = act.activation(probs[:, p, seq(b)], ps_s[:, seq(b)], ACT.Exp,
                                          bias=neg_max[:, p, b:b + 1],
                                          accum_out=row_sum[:, p, b:b + 1])
                last.then_inc(probs_ready, 1)

            def phase_a(i, p):
                q = 1 - p
                if inside(i) and not (isinstance(i, int) and i == 0):
                    softmax(i, p)
                if inside(i + 1):
                    act.wait_ge(q_done, i + 2)
                    reuse(act, scores_done, i)
                    act.activation(qT[:, q, :], ps_q[:], ACT.Identity, bias=bq_scaled[:],
                                   scale=SCALE).then_inc(qT_ready, 1)
                    act.wait_ge(k_done, i + 2)
                    act.activation(kT[:, q, :], ps_k[:], ACT.Identity, bias=col_a(BK)).then_inc(kT_ready, 1)
                    if isinstance(i, int) and i == -1:
                        act.dma_start(w2[:], W2.rearrange("(k p) d -> p k d", p=P)).then_inc(w2_in, 16)
                        modulate1(1, 1)
                    act.wait_ge(v_done, i + 2)
                    reuse(act, o_done, i)
                    act.activation(v_tok[:, q, :], ps_v[:], ACT.Copy).then_inc(v_ready, 1)
                    if isinstance(i, int) and i == -1:
                        softmax(0, 0)
                if isinstance(i, int) and i == G - 1:
                    act.preload_act_table(ACT.Gelu)
                    gelu1(0)
                    modulate2(1)
                if inside(i):
                    act.wait_ge(pT_done, i + 1)
                    act.activation(pT[:, p, :], ps_pT[:], ACT.Copy).then_inc(pT_ready, 1)
                if inside(i + 2) and not (isinstance(i, int) and i == -1):
                    modulate1(i + 2, p)
                elif isinstance(i, int) and i == G - 2:
                    act.wait_ge(mod2_ready, 3)
                    modulate2(0)

            def phase_b(i, p):
                if isinstance(i, int) and i == G - 1:
                    for h in range(2):
                        act.wait_ge(y_done, G + h)
                        act.activation(act2[:, p, half_of(h)], ps_y_half[h][:, half_of(h)], ACT.Gelu,
                                       bias=col_b(B2)).then_inc(act2_ready, 1)
                    return
                if inside(i):
                    act.wait_ge(y_done, i + 1)
                    act.activation(act2[:, p, :], ps_y[:], ACT.Gelu, bias=col_b(B2)).then_inc(act2_ready, 1)
                if inside(i + 1):
                    gelu1(i + 1)
                if inside(i + 2):
                    modulate2(i + 2)
                if inside(i):
                    act.wait_ge(act2_ready, i + 1)
                    reuse(act, oT_done, i)
                    for b in range(GB):
                        last = act.activation(act2_gated[:, seq(b)], act2[:, p, seq(b)], ACT.Copy,
                                              scale=a2[:, ds(i * GB + b, 1)])
                    last.then_inc(gated_ready, 1)

            act.preload_act_table(ACT.Exp)
            act.dma_start(wc[:, :, A2 * P:MC * P], wc_dram[:, :, A2 * P:MC * P]).then_inc(wc_rest_in, 16)
            act.wait_ge(mod1_ready, 2)
            modulate1(0, 0)
            act.wait_ge(bq_ready, 1)
            steps(act, phase_a, -1, G - 1)
            steps(act, phase_b, 0, G - 1)

        @block.vector
        def _(dve):
            def stats1(g, p):
                dve.wait_ge(x_in[p], dma_count(g, p))
                for b in range(GB):
                    last = dve.bn_stats(stats[:, p, b, :], x_all[:, ds(g * GW + b * P, P)])
                last.then_inc(stats_done, 1)

            def aggregate1(g, p):
                for b in range(GB):
                    last = dve.bn_aggr(moments[:, p, b, :], stats[:, p, b, :])
                last.then_inc(moments_ready, 1)

            def normalize1(g, p, x1_of=None):
                dve.wait_ge(rstd_ready, g + 1)
                reuse(dve, nT_ready, g - 1)
                for b in range(GB):
                    last = dve.tensor_scalar(n_tok[:, p, seq(b)], x_all[:, ds(g * GW + b * P, P)],
                                             moments[:, p, b, 0:1], rstd[:, p, b:b + 1],
                                             ALU.subtract, ALU.mult)
                    if b == 0 and x1_of is not None:
                        dve.wait_ge(x1_ready, x1_of + 1)
                last.then_inc(n_ready, 1)

            def split_h2(g):
                dve.wait_ge(h2_ready, g + 1)
                reuse(dve, hid_done, HC * g)
                dve.tensor_copy(h2_hi[:], h2[:]).then_inc(h2_hi_ready, 1)
                dve.wait_ge(h2_hi_ready, g + 1)
                dve.tensor_tensor(h2_lo[:], h2[:], h2_hi[:].bitcast(F32), ALU.subtract).then_inc(h2_split, 1)

            def split_act1(g):
                def high(j):
                    dve.wait_ge(act1_ready, HC * g + j + 1)
                    dve.tensor_copy(act1_hi[:, j, :], act1[:, j, :]).then_inc(act1_hi_ready, 1)

                def low(j):
                    dve.wait_ge(act1_hi_ready, HC * g + j + 1)
                    dve.tensor_tensor(act1_lo[:, j, :], act1[:, j, :], act1_hi[:, j, :].bitcast(F32),
                                      ALU.subtract).then_inc(act1_lo_dve, 1)

                high(0)
                high(1)
                low(0)
                for j in range(2, HC):
                    high(j)
                for j in DVE_CHUNKS[1:]:
                    low(j)

            def invert_sums(g, p):
                dve.wait_ge(probs_ready, g + 1)
                dve.reciprocal(inv_sum[:, p, :], row_sum[:, p, :]).then_inc(inv_ready, 1)

            def aggregate2(g, p):
                for b in range(GB):
                    last = dve.bn_aggr(moments2[:, p, b, :], stats2[:, p, b, :])
                last.then_inc(moments2_ready, 1)

            def add_attention(g, p):
                dve.wait_ge(inv_ready, g + 1)
                dve.wait_ge(x_bias_ready, g + 1)
                dve.wait_ge(o_done, g + 1)
                for b in range(GB):
                    last = dve.scalar_tensor_tensor(x1_all[:, ds(g * GW + b * P, P)],
                                                    ps_o[:, seq(b)], inv_sum[:, p, b:b + 1],
                                                    x_bias[:, p, seq(b)], ALU.mult, ALU.add)
                last.then_inc(x1_ready, 1)

            def stats2_of(g, p):
                for b in range(GB):
                    last = dve.bn_stats(stats2[:, p, b, :], x1_all[:, ds(g * GW + b * P, P)])
                last.then_inc(stats2_done, 1)

            def phase_a(i, p):
                q = 1 - p
                ahead = inside(i + 2) and not (isinstance(i, int) and i == 0)
                if ahead:
                    stats1(i + 2, p)
                    dve.wait_ge(stats_done, i + 3)
                if inside(i - 2):
                    dve.wait_ge(stats2_done, i - 1)
                    if isinstance(i, int):
                        reuse(dve, rstd2_ready, i - 3)
                if isinstance(i, int) and i == 1:
                    dve.wait_ge(w2_in, 16)
                    dve.tensor_copy(w2_hi[:], w2[:]).then_inc(w2_hi_ready, 1)
                dve.wait_ge(scores_done, i + 1)
                reuse(dve, probs_ready, i - 1)
                dve.tensor_reduce(neg_max[:, p, :], ps_s[:].rearrange("s (b t) -> s b t", b=GB),
                                  AX_X, ALU.max, negate=True).then_inc(max_ready, 1)
                if isinstance(i, int) and i == G - 1:
                    split_h2(0)
                if inside(i - 1):
                    invert_sums(i - 1, q)
                if ahead:
                    aggregate1(i + 2, p)
                if inside(i - 2):
                    aggregate2(i - 2, p)
                if isinstance(i, int) and i == 0:
                    modulation2()
                    dve.wait_ge(w1_in, 16)
                    dve.tensor_copy(w1_hi[:], w1[:]).then_inc(w1_hi_ready, 1)
                if inside(i - 1):
                    add_attention(i - 1, q)
                if inside(i + 2):
                    normalize1(i + 2, p, i - 1 if inside(i - 1) else None)
                elif inside(i - 1):
                    dve.wait_ge(x1_ready, i)
                if inside(i - 1):
                    stats2_of(i - 1, q)

            def gain(n, m):
                return dve.tensor_scalar(one_g[:, n, :], cond(m), col_a(BC + m), 1.0, ALU.add, ALU.add)

            def modulation2():
                dve.wait_ge(cols_b_T, 1)
                dve.tensor_copy(cols_b[:], ps_late[:, cols_b_at:cols_b_at + NB]).then_inc(cols_b_ready, 1)
                dve.wait_ge(cols_b_ready, 1)
                dve.wait_ge(cond2_done, 1)
                gain(1, G2).then_inc(mod2_step, 1)
                dve.wait_ge(mod2_step, 1)
                dve.tensor_scalar(scale2[:], one_g[:, 1, :], col_b(LG2), None, ALU.mult).then_inc(mod2_ready, 1)
                dve.tensor_scalar(shift_part[:, 1, :], one_g[:, 1, :], col_b(LB2), None,
                                  ALU.mult).then_inc(mod2_step, 1)
                dve.wait_ge(mod2_step, 2)
                dve.scalar_tensor_tensor(shift2[:], cond(BE2), col_a(BC + BE2), shift_part[:, 1, :],
                                         ALU.add, ALU.add).then_inc(mod2_ready, 1)
                dve.tensor_scalar(a2[:], cond(A2), col_a(BC + A2), None, ALU.add).then_inc(mod2_ready, 1)

            def phase_b(i, p):
                q = 1 - p
                if inside(i + 1):
                    split_act1(i + 1)
                if inside(i + 2):
                    split_h2(i + 2)
                if isinstance(i, int) and i == 0:
                    dve.wait_ge(x1_ready, G)
                    stats2_of(G - 1, 1)
                    dve.wait_ge(rstd2_ready, G - 2)
                    dve.wait_ge(stats2_done, G)
                    aggregate2(G - 1, 1)
                if isinstance(i, int) and i == G - 1:
                    dve.wait_ge(oT_done, G - 1)
                    for h in range(2):
                        dve.wait_ge(act2_ready, G + h)
                        for b in range(h * GB // 2, (h + 1) * GB // 2):
                            last = dve.tensor_scalar(act2_gated[:, seq(b)], act2[:, p, seq(b)],
                                                     a2[:, (G - 1) * GB + b:(G - 1) * GB + b + 1], None, ALU.mult)
                        last.then_inc(gated_half, 1)
                if isinstance(i, int) and i == G:
                    for h in range(2):
                        dve.wait_ge(oT_done, G + h)
                        dve.tensor_tensor(out_last[:, half_of(h)], ps_oT_half[h][:, half_of(h)],
                                          x1_all[:, ds((G - 1) * GW + h * GW // 2, GW // 2)],
                                          ALU.add).then_inc(out_ready, 1)
                elif inside(i - 1):
                    dve.wait_ge(oT_done, i)
                    dve.wait_ge(stored[q], dma_count(i - 1, q))
                    dve.tensor_tensor(out_tok[:, q, :], ps_oT[:], x1_all[:, ds((i - 1) * GW, GW)],
                                      ALU.add).then_inc(out_ready, 1)

            dve.wait_ge(tc_done, 1)
            dve.tensor_copy(tc_T[:].rearrange("p k b -> p (k b)"), ps_tc[:, 0:KC * B]).then_inc(tc_ready, 1)
            stats1(0, 0)
            dve.wait_ge(stats_done, 1)
            aggregate1(0, 0)
            dve.wait_ge(gate_done, 1)
            dve.tensor_copy(gate_rows[:, 0, :], ps_gate[0:B, 0:P])
            dve.wait_ge(bv_row_in, 16)
            dve.tensor_tensor(gate_rows[:, 1, :], ps_gate[0:B, 0:P], bv_row[:], ALU.mult)\
                .then_inc(gate_rows_ready, 1)
            dve.wait_ge(cols_a_T, 1)
            dve.tensor_copy(cols_a[:], ps_vec[:, 0:NA]).then_inc(cols_a_ready, 1)
            normalize1(0, 0)
            dve.wait_ge(cols_a_ready, 1)
            dve.wait_ge(cond1_done, 1)
            gain(0, G1).then_inc(mod1_step, 1)
            dve.wait_ge(mod1_step, 1)
            dve.tensor_scalar(scale1[:], one_g[:, 0, :], col_a(LG1), None, ALU.mult).then_inc(mod1_ready, 1)
            dve.tensor_scalar(shift_part[:, 0, :], one_g[:, 0, :], col_a(LB1), col_a(BC + BE1), ALU.mult,
                              ALU.add).then_inc(mod1_step, 1)
            dve.wait_ge(mod1_step, 2)
            dve.tensor_tensor(shift1[:], cond(BE1), shift_part[:, 0, :], ALU.add).then_inc(mod1_ready, 1)
            dve.tensor_scalar(bq_scaled[:], col_a(BQ), SCALE, None, ALU.mult).then_inc(bq_ready, 1)
            stats1(1, 1)
            dve.wait_ge(stats_done, 2)
            aggregate1(1, 1)
            normalize1(1, 1)
            stats1(2, 0)
            dve.wait_ge(stats_done, 3)
            aggregate1(2, 0)
            steps(dve, phase_a, 0, G - 1)
            split_act1(0)
            split_h2(1)
            invert_sums(G - 1, 1)
            dve.wait_ge(stats2_done, G - 1)
            dve.wait_ge(rstd2_ready, G - 3)
            aggregate2(G - 2, 0)
            add_attention(G - 1, 1)
            steps(dve, phase_b, 0, G)

        @block.tensor
        def _(pe):
            def transpose_group(dest, src, done):
                for b in range(GB):
                    last = pe.transpose(dest[:, seq(b)], src[:, seq(b)], ident[:])
                last.then_inc(done, 1)


            def transpose_n1(g, p):
                pe.wait_ge(n_ready, g + 1)
                reuse(pe, hT_ready, 2 * g)
                transpose_group(ps_nT, n_tok[:, p, :], nT_ready)

            def transpose_n2(g, p):
                pe.wait_ge(n2_ready, g + 1)
                reuse(pe, h2_ready, g)
                transpose_group(ps_n2T, n2_tok[:, p, :], n2T_ready)

            def up(g):
                pe.wait_ge(h2_hi_ready, g + 1)
                for j in range(HC):
                    pe.matmul(ps_hid[j][:], w1_lo[:, seq(j)], h2_hi[:], start=True, stop=False)
                    pe.matmul(ps_hid[j][:], w1_hi[:, seq(j)], h2_hi[:], start=False, stop=False)
                    if j == 0:
                        pe.wait_ge(h2_split, g + 1)
                    pe.matmul(ps_hid[j][:], w1_hi[:, seq(j)], h2_lo[:], start=False, stop=True)\
                        .then_inc(hid_done, 1)

            def transpose_gated(g):
                pe.wait_ge(gated_ready, g + 1)
                reuse(pe, out_ready, g)
                transpose_group(ps_oT, act2_gated, oT_done)

            def down(g, parts):
                def columns(n):
                    return slice(n * GW // len(parts), (n + 1) * GW // len(parts))

                reuse(pe, act2_ready, g)
                for j in range(HC):
                    pe.wait_ge(act1_hi_ready, HC * g + j + 1)
                    for w in (w2_lo, w2_hi):
                        for n, y in enumerate(parts):
                            pe.matmul(y[:, columns(n)], w[:, j, :], act1_hi[:, j, columns(n)],
                                      start=j == 0 and w is w2_lo, stop=False)
                for n, y in enumerate(parts):
                    for j in range(HC):
                        for chunks, ready in ((DVE_CHUNKS, act1_lo_dve), (POOL_CHUNKS, act1_lo_pool)):
                            if n == 0 and j in chunks:
                                pe.wait_ge(ready, len(chunks) * g + chunks.index(j) + 1)
                        last = pe.matmul(y[:, columns(n)], w2_hi[:, j, :], act1_lo[:, j, columns(n)],
                                         start=False, stop=j == HC - 1)
                    last.then_inc(y_done, 1)

            def score(g, p):
                pe.wait_ge(qT_ready, g + 1)
                pe.wait_ge(kT_ready, g + 1)
                reuse(pe, probs_ready, g)
                for b in range(GB):
                    last = pe.matmul(ps_s[:, seq(b)], qT[:, p, seq(b)], kT[:, p, seq(b)],
                                     start=True, stop=True)
                last.then_inc(scores_done, 1)

            def attend(g, p):
                pe.wait_ge(pT_ready, g + 1)
                pe.wait_ge(v_ready, g + 1)
                reuse(pe, x1_ready, g)
                for b in range(GB):
                    last = pe.matmul(ps_o[:, seq(b)], pT[:, p, seq(b)], v_tok[:, p, seq(b)],
                                     start=True, stop=True)
                last.then_inc(o_done, 1)

            def project_cond(m):
                for k in range(KC):
                    last = pe.matmul(cond(m), wc[:, k, seq(m)], tc_T[:, k, :],
                                     start=k == 0, stop=k == KC - 1)
                return last

            def phase_a(i, p):
                q = 1 - p
                if inside(i) and not (isinstance(i, int) and i == 0):
                    score(i, p)
                if inside(i - 1):
                    if isinstance(i, int) and i == 1:
                        pe.wait_ge(mod2_ready, 3)
                    attend(i - 1, q)
                if inside(i + 1):
                    reuse(pe, qT_ready, i + 1)
                    for half in range(2):
                        cols = half_of(half)
                        pe.wait_ge(hT_ready, 2 * (i + 1) + half + 1)
                        last = pe.matmul(ps_q[:, cols], wq[:], hT[:, q, cols], start=True, stop=True)
                    last.then_inc(q_done, 1)
                    reuse(pe, kT_ready, i + 1)
                    pe.matmul(ps_k[:], wk[:], hT[:, q, :], start=True, stop=True).then_inc(k_done, 1)
                    if isinstance(i, int) and i == -1:
                        pe.wait_ge(wc_rest_in, 16)
                        for m in (A2, G2, BE2):
                            last = project_cond(m)
                        last.then_inc(cond2_done, 1)
                        transpose_n1(1, 1)
                        score(0, 0)
                    pe.wait_ge(wv_gated_ready, i + 2)
                    reuse(pe, v_ready, i + 1)
                    for b in range(GB):
                        last = pe.matmul(ps_v[:, seq(b)], hT[:, q, seq(b)], wv_gated[:, q, seq(b)],
                                         start=True, stop=True)
                    last.then_inc(v_done, 1)
                if isinstance(i, int) and i == G - 1:
                    pe.wait_ge(v_ready, G)
                    pe.wait_ge(w_split, 2)
                    up(0)
                    transpose_n2(1, 1)
                if inside(i):
                    pe.wait_ge(probs_ready, i + 1)
                    reuse(pe, pT_ready, i)
                    transpose_group(ps_pT, probs[:, p, :], pT_done)
                if inside(i + 2) and not (isinstance(i, int) and i == -1):
                    transpose_n1(i + 2, p)
                elif isinstance(i, int) and i == G - 2:
                    transpose_n2(0, 0)

            def phase_b(i, p):
                if inside(i):
                    down(i, ps_y_half if isinstance(i, int) and i == G - 1 else (ps_y,))
                if isinstance(i, int) and i == 0:
                    attend(G - 1, 1)
                if inside(i + 1):
                    up(i + 1)
                if inside(i + 2):
                    transpose_n2(i + 2, p)
                if isinstance(i, int) and i == G:
                    for h in range(2):
                        pe.wait_ge(gated_half, h + 1)
                        for b in range(h * GB // 2, (h + 1) * GB // 2):
                            last = pe.transpose(ps_oT_half[h][:, seq(b)], act2_gated[:, seq(b)], ident[:])
                        last.then_inc(oT_done, 1)
                elif inside(i - 1):
                    transpose_gated(i - 1)

            def keep_warm(count):
                for _ in range(count):
                    pe.matmul(ps_v[:, 0:P], ident[:], ident[:], start=True, stop=True)

            pe.wait_ge(consts_ready, 1)
            keep_warm(WARM[0])
            pe.wait_ge(tc_in, 32)
            for k in range(KC):
                last = pe.transpose(ps_tc[:, k * B:(k + 1) * B], tc_rows[:, k, :], ident[0:B, 0:B])
            last.then_inc(tc_done, 1)
            keep_warm(WARM[1])
            pe.wait_ge(tc_ready, 1)
            pe.wait_ge(wc_gate_in, 16)
            for k in range(KC):
                pe.matmul(ps_gate[0:B, 0:P], tc_T[:, k, :], wc[:, k, seq(A1)], start=k == 0, stop=False)
            pe.wait_ge(bc_in, 16)
            pe.matmul(ps_gate[0:B, 0:P], ones_row[:], rows_a[BC + A1:BC + A1 + 1, :], start=False,
                      stop=True).then_inc(gate_done, 1)
            keep_warm(WARM[2])
            pe.wait_ge(cols_a_in, 16 * 2)
            pe.wait_ge(bqk_in, 16 * 2)
            pe.transpose(ps_vec[:, 0:NA], rows_a[:], ident[0:NA, 0:NA]).then_inc(cols_a_T, 1)
            pe.wait_ge(wc_mod1_in, 16)
            project_cond(G1)
            project_cond(BE1).then_inc(cond1_done, 1)
            keep_warm(WARM[3])
            transpose_n1(0, 0)
            keep_warm(WARM[4])
            pe.wait_ge(qk_in, 32)
            phase_a(-1, 1)
            pe.wait_ge(cols_b_in, 16 * 2)
            pe.wait_ge(ln2_in, 16 * 2)
            pe.transpose(ps_late[:, cols_b_at:cols_b_at + NB], rows_b[:], ident[0:NB, 0:NB])\
                .then_inc(cols_b_T, 1)
            steps(pe, phase_a, 0, G - 1)
            steps(pe, phase_b, 0, G)


_INS = ["x", "fside_BxS_0", "cond_1024"] + [
    "L0_cond_" + n for n in ("Wq", "bq", "Wk", "bk", "Wv", "bv", "W1", "b1", "W2", "b2", "Wc", "bc",
                             "ln1_g", "ln1_b", "ln2_g", "ln2_b")]


def kernel(**inputs):
    import numpy as _np
    import concourse.bacc as _bacc
    from concourse import mybir as _mybir
    from concourse.bass_utils import run_bass_kernel_spmd as _run

    nc = _bacc.Bacc("TRN2", target_bir_lowering=False, num_devices=1)
    arrays, args = {}, []
    for name in _INS:
        a = _np.ascontiguousarray(inputs[name])
        arrays[f"in_{name}"] = a
        args.append(nc.dram_tensor(f"in_{name}", a.shape, _mybir.dt.from_np(a.dtype), kind="ExternalInput").ap())
    out = nc.dram_tensor("out_x", arrays["in_x"].shape, _mybir.dt.float32, kind="ExternalOutput").ap()
    cond_block_kernel(nc, *args, out)
    r = _run(nc, [arrays], core_ids=[0])
    return r.results[0]["out_x"]
```
